# Optimizing a Trainium2 kernel written in Bass

```python
import numpy as np
import jax
import jax.numpy as jnp

def _softmax(x, axis=-1):
    return jax.nn.softmax(x, axis=axis)

def _gelu(x):
    return jax.nn.gelu(x, approximate=True)

def _silu(x):
    return jax.nn.silu(x)

def _sigmoid(x):
    return jax.nn.sigmoid(x)

def _layernorm(x, axis=-1, eps=1e-05):
    m = jnp.mean(x, axis=axis, keepdims=True)
    v = jnp.var(x, axis=axis, keepdims=True)
    return (x - m) / jnp.sqrt(v + eps)

def _scatter_add(tgt, idx, src, axis=0):
    return tgt.at[idx].add(src)

def _segment_sum(src, seg, n):
    return jax.ops.segment_sum(src, seg, n)
kernel_name = 'mk_flamingo_gated_d1_seqx_r2_95726f'

def setup_inputs(seed: int=0):
    np.random.seed(seed)
    _w = jnp.asarray

    def _rec_inputs():
        import jax
        import jax.numpy as jnp
        _rk = jax.random.key(seed)
        x = 7.22e-05 + 1 * jax.random.normal(jax.random.fold_in(_rk, 1), (64, 256, 512), jnp.float32)
        _lenS = 256 - jax.random.randint(jax.random.fold_in(_rk, 7), (64,), 0, max(1, 256 // 4) + 1, jnp.int32)
        _lenS2 = 256 - jax.random.randint(jax.random.fold_in(_rk, 8), (64,), 0, max(1, 256 // 4) + 1, jnp.int32)
        _ctx_1024P = jax.random.normal(jax.random.fold_in(_rk, 11), (64, 16, 512), jnp.float32)
        _ctx_1024c = jax.random.dirichlet(jax.random.fold_in(_rk, 511), 0.3 * jnp.ones((16,), jnp.float32), (64, 256))
        _ctx_1024t = jnp.einsum('bsk,bkd->bsd', _ctx_1024c, _ctx_1024P)
        _ctx_1024t = _ctx_1024t * jax.lax.rsqrt(jnp.mean(jnp.square(_ctx_1024t)) + 1e-12) * 0.953939
        ctx_1024 = 4.13588e-05 + 0.999923 * (_ctx_1024t + 0.3 * jax.random.normal(jax.random.fold_in(_rk, 611), (64, 256, 512), jnp.float32))
        _g = jax.random.normal(jax.random.fold_in(_rk, 9001), (2, 1), jnp.float32)
        _g = jnp.sign(_g) * jnp.maximum(jnp.abs(_g), 1.0) + (_g == 0) * 1.0
        g_xattn = _g[0]
        g_ffn = _g[1]
        return (x, ctx_1024, g_xattn, g_ffn)
    x, ctx_1024, g_xattn, g_ffn = _rec_inputs()

    def _L0_xattn_setup():
        import jax, jax.numpy as jnp
        import numpy as np
        NUM_HEADS = 16
        DIM_M = 512
        key = jax.random.key(seed)
        kq, kk, kv, kw, kb = jax.random.split(key, 5)
        B, T, D = (4, 1024, DIM_M)
        q = jax.random.normal(kq, (B, T, D), dtype=jnp.float32)
        k = jax.random.normal(kk, (B, T, D), dtype=jnp.float32)
        v = jax.random.normal(kv, (B, T, D), dtype=jnp.float32)
        lim = 1.0 / np.sqrt(D)
        ffn_w = jax.random.uniform(kw, (D, D), jnp.float32, -lim, lim)
        ffn_b = jax.random.uniform(kb, (D,), jnp.float32, -lim, lim)
        return {'q': q, 'k': k, 'v': v, 'ffn_w': ffn_w, 'ffn_b': ffn_b}
    _L0_xattn_all = _L0_xattn_setup()
    _L0_xattn_in = {k: v for k, v in _L0_xattn_all.items() if k in ('ffn_w', 'ffn_b')}
    del _L0_xattn_all

    def _L0_ffn_setup():
        import jax, jax.numpy as jnp
        import numpy as np
        DIM = 512

        def _reference_tuple_inner(x, W_r, W_k, W_v, mu_r, mu_k):
            B, T, C = x.shape
            x_prev = jnp.concatenate([jnp.zeros((B, 1, C), x.dtype), x[:, :-1, :]], axis=1)
            xr = mu_r * x + (1.0 - mu_r) * x_prev
            xk = mu_k * x + (1.0 - mu_k) * x_prev
            r = jax.nn.sigmoid(jnp.einsum('btc,dc->btd', xr, W_r))
            k = jnp.einsum('btc,dc->btd', xk, W_k)
            k_act = jnp.square(jax.nn.relu(k))
            out = r * jnp.einsum('btc,dc->btd', k_act, W_v)
            new_state = x[:, -1, :]
            return (out, new_state)
        key = jax.random.key(seed)
        ks = jax.random.split(key, 6)
        B, T, C = (8, 1024, DIM)
        x = jax.random.normal(ks[0], (B, T, C), dtype=jnp.float32)
        s = 1.0 / np.sqrt(C)
        W_r = jax.random.uniform(ks[1], (C, C), jnp.float32, -s, s)
        W_k = jax.random.uniform(ks[2], (C, C), jnp.float32, -s, s)
        W_v = jax.random.uniform(ks[3], (C, C), jnp.float32, -s, s)
        mu_r = jax.random.uniform(ks[4], (C,), jnp.float32)
        mu_k = jax.random.uniform(ks[5], (C,), jnp.float32)
        return {'x': x, 'W_r': W_r, 'W_k': W_k, 'W_v': W_v, 'mu_r': mu_r, 'mu_k': mu_k}
    _L0_ffn_all = _L0_ffn_setup()
    _L0_ffn_in = {k: v for k, v in _L0_ffn_all.items() if k in ('W_r', 'W_k', 'W_v', 'mu_r', 'mu_k')}
    del _L0_ffn_all
    return {'x': x, 'ctx_1024': ctx_1024, 'g_xattn': g_xattn, 'g_ffn': g_ffn, 'L0_xattn_ffn_w': _L0_xattn_in['ffn_w'], 'L0_xattn_ffn_b': _L0_xattn_in['ffn_b'], 'L0_ffn_W_r': _L0_ffn_in['W_r'], 'L0_ffn_W_k': _L0_ffn_in['W_k'], 'L0_ffn_W_v': _L0_ffn_in['W_v'], 'L0_ffn_mu_r': _L0_ffn_in['mu_r'], 'L0_ffn_mu_k': _L0_ffn_in['mu_k']}

def reference(x, ctx_1024, g_xattn, g_ffn, L0_xattn_ffn_w, L0_xattn_ffn_b, L0_ffn_W_r, L0_ffn_W_k, L0_ffn_W_v, L0_ffn_mu_r, L0_ffn_mu_k):
    import jax
    import jax.numpy as jnp

    def _L0_xattn_ref(q, k, v, ffn_w, ffn_b):
        import jax, jax.numpy as jnp
        import numpy as np
        NUM_HEADS = 16
        DIM_M = 512
        bs, ts, fq = q.shape
        h = NUM_HEADS
        hd = fq // h
        qs = jax.nn.relu(q.reshape(bs, ts, h, hd))
        ks = jax.nn.relu(k.reshape(bs, ts, h, hd))
        vs = jax.nn.relu(v.reshape(bs, ts, h, hd))
        att = jnp.einsum('bthf,byhf->bhty', qs, ks)
        att = jax.nn.softmax(att / jnp.sqrt(jnp.float32(hd)), axis=-1)
        out = jnp.einsum('bhty,byhf->bhtf', att, vs)
        out = out.reshape(bs, ts, -1)
        return jax.nn.relu(out @ ffn_w.T + ffn_b)

    def _L0_ffn_ref(x, W_r, W_k, W_v, mu_r, mu_k):
        import jax, jax.numpy as jnp
        import numpy as np
        DIM = 512

        def _reference_tuple_inner(x, W_r, W_k, W_v, mu_r, mu_k):
            B, T, C = x.shape
            x_prev = jnp.concatenate([jnp.zeros((B, 1, C), x.dtype), x[:, :-1, :]], axis=1)
            xr = mu_r * x + (1.0 - mu_r) * x_prev
            xk = mu_k * x + (1.0 - mu_k) * x_prev
            r = jax.nn.sigmoid(jnp.einsum('btc,dc->btd', xr, W_r))
            k = jnp.einsum('btc,dc->btd', xk, W_k)
            k_act = jnp.square(jax.nn.relu(k))
            out = r * jnp.einsum('btc,dc->btd', k_act, W_v)
            new_state = x[:, -1, :]
            return (out, new_state)
        return _reference_tuple_inner(x, W_r, W_k, W_v, mu_r, mu_k)[0]
    x = x + jnp.tanh(g_xattn[0]) * _L0_xattn_ref(_layernorm(x, axis=-1), ctx_1024, ctx_1024, L0_xattn_ffn_w, L0_xattn_ffn_b)
    x = x + jnp.tanh(g_ffn[0]) * _L0_ffn_ref(_layernorm(x, axis=-1), L0_ffn_W_r, L0_ffn_W_k, L0_ffn_W_v, L0_ffn_mu_r, L0_ffn_mu_k)
    return x

_drawn_inputs = setup_inputs


def setup_inputs(seed=0):
    import zlib

    import numpy as np

    out = dict(_drawn_inputs(seed))
    spreads = {}
    factors = {'L0_xattn_ffn_b': 4.203, 'L0_ffn_W_r': 3.364, 'L0_ffn_mu_r': 6.958}
    for name, (base, spread) in spreads.items():
        noise = np.random.default_rng([zlib.crc32(name.encode()), seed]).standard_normal(out[name].shape)
        drawn = base * np.exp(spread * noise) if base else spread * noise
        out[name] = jnp.asarray(drawn.astype(out[name].dtype))
    for name, factor in factors.items():
        out[name] = (out[name] * factor).astype(out[name].dtype)
    return out
```

```python
from contextlib import ExitStack

import concourse.bass as bass
from concourse import mybir

F32 = mybir.dt.float32
F32R = mybir.dt.float32r
ALU = mybir.AluOpType
ACT = mybir.ActivationFunctionType
AX_X = mybir.AxisListType.X

P = 128
HEADS = 16
LN_EPS = 1e-5


def flamingo_block(nc, x, ctx_in, ctx_t, g_xattn, g_ffn, w_t, bias, mu, out):
    NB, T, D = x.shape
    HD = D // HEADS
    NU = T // P
    KC = D // P
    GR = P // HD
    CH = HEADS // GR
    STEPS = HEADS
    SCALE = float(HD) ** -0.5
    assert NU == 2 and KC == 4 and GR == 4 and CH == 4 and HD == 32
    QK = 3 * HD
    ST = QK + 2
    AHEAD = 6

    es = ExitStack()
    with es:
        def sb(name, shape, dt=F32):
            return es.enter_context(nc.sbuf_tensor(name, shape, dt))

        def sem(name):
            return es.enter_context(nc.semaphore(name))

        o_dram = nc.dram_tensor("o_dram", [CH, GR, HD, GR, T // GR], F32, kind="Internal").ap()

        w_hi = [sb(f"w_hi{n}", [P, KC, D], F32R) for n in range(4)]
        w_lo = [sb(f"w_lo{n}", [P, KC, D], F32R) for n in range(4)]
        W_X, W_R, W_K, W_V = range(4)
        x_ln = sb("x_ln", [P, NU, D])
        q_nat = sb("q_nat", [P, NU, HEADS, 3, HD], F32R)
        v_pos = sb("v_pos", [P, 2, NU, D])
        k_raw = sb("k_raw", [P, GR, T])
        k_st = sb("k_st", [P, CH, GR, T], F32R)
        q_st = sb("q_st", [P, CH, GR, T], F32R)
        probs = sb("probs", [P, 2, GR, NU, T])
        o_val = sb("o_val", [P, T])
        o_mv = sb("o_mv", [P, 2 * GR, T // GR])
        o_hi = sb("o_hi", [P, KC, T], F32R)
        o_lo = sb("o_lo", [P, KC, T], F32R)
        x1 = sb("x1", [P, 2, NU, D])
        xn = sb("xn", [P, NU, D])
        xt = sb("xt", [P, KC, T + 1])
        xd = sb("xd", [P, KC, T])
        xm = sb("xm", [P, KC, T])
        xr_hi = sb("xr_hi", [P, KC, T], F32R)
        xr_lo = sb("xr_lo", [P, KC, T], F32R)
        xk_hi = sb("xk_hi", [P, KC, T], F32R)
        xk_lo = sb("xk_lo", [P, KC, T], F32R)
        ka_hi = sb("ka_hi", [P, KC, T], F32R)
        ka_lo = sb("ka_lo", [P, KC, T], F32R)
        th = sb("th", [P, NU, D])
        b_rows = sb("b_rows", [P, D], F32R)
        ones_r = sb("ones_r", [P, P], F32R)
        ident_r = sb("ident_r", [P, P], F32R)
        m_t = sb("m_t", [P, T], F32R)
        nmax = sb("nmax", [P, NU, GR])
        m_nat = sb("m_nat", [P, NU, 2, GR], F32R)
        st6 = sb("st6", [P, 2, NU, 6])
        mv = sb("mv", [P, 2, NU, 2])
        ve = sb("ve", [P, 2, NU])
        rstd = sb("rstd", [P, 2, NU])
        carrier = sb("carrier", [P, 1])
        mhalf = sb("mhalf", [P, 1])
        mu_sb = sb("mu_sb", [P, 2, KC])
        gates = sb("gates", [P, 2])
        tg = sb("tg", [P, 2])
        tgh = sb("tgh", [P, 1])
        w_raw = probs[:, :, :, :, :].rearrange("p a g v t -> p (a g v t)")[:, 0:KC * D]
        ident_raw = xn[:, 0, 0:P]
        b_raw = th[0:1, 0, :]
        b_low = th[0:1, 1, :].bitcast(F32R)

        bank = [es.enter_context(nc.psum_tensor(f"bank{n}", [P, 512], F32)) for n in range(8)]
        s_bank, st_bank, pv_bank, dense_bank, tp_bank = bank[0:2], bank[2:4], bank[4], bank[5:7], bank[7]

        x_loaded = sem("x_loaded")
        v_loaded = [sem("v_loaded0"), sem("v_loaded1")]
        k_loaded = sem("k_loaded")
        x1_loaded = sem("x1_loaded")
        m_moved = [sem("m_moved0"), sem("m_moved1")]
        stored = sem("stored")
        setup_loaded = sem("setup_loaded")
        w_loaded = sem("w_loaded")
        setup_pool = sem("setup_pool")
        setup_ones = sem("setup_ones")
        setup_act = sem("setup_act")
        setup_dve = sem("setup_dve")
        b_low_moved = sem("b_low_moved")
        var_ready = sem("var_ready")
        rstd_ready = sem("rstd_ready")
        x_normed = sem("x_normed")
        q_hi_ready = sem("q_hi_ready")
        q_lo_ready = sem("q_lo_ready")
        q_turned = sem("q_turned")
        q_stacked = sem("q_stacked")
        v_ready = sem("v_ready")
        k_pos = sem("k_pos")
        k_hi_ready = sem("k_hi_ready")
        k_lo_ready = sem("k_lo_ready")
        s_ready = sem("s_ready")
        s_maxed = sem("s_maxed")
        m_hi_ready = sem("m_hi_ready")
        m_split = sem("m_split")
        m_turned = sem("m_turned")
        m_copied = sem("m_copied")
        st_ready = sem("st_ready")
        exp_ready = sem("exp_ready")
        pv_ready = sem("pv_ready")
        rden_ready = sem("rden_ready")
        o_ready = sem("o_ready")
        o_written = sem("o_written")
        o_moved = sem("o_moved")
        o_hi_ready = sem("o_hi_ready")
        o_lo_ready = sem("o_lo_ready")
        z_ready = sem("z_ready")
        z_relued = sem("z_relued")
        x1_ready = sem("x1_ready")
        stat2 = sem("stat2")
        mv2 = sem("mv2")
        stat1 = sem("stat1")
        mv1 = sem("mv1")
        var2_ready = sem("var2_ready")
        rstd2_ready = sem("rstd2_ready")
        xn_ready = sem("xn_ready")
        xn_turned = sem("xn_turned")
        xt_ready = sem("xt_ready")
        xd_ready = sem("xd_ready")
        xk_ready = sem("xk_ready")
        xk_hi_ready = sem("xk_hi_ready")
        xk_lo_ready = sem("xk_lo_ready")
        xr_ready = sem("xr_ready")
        xr_hi_ready = sem("xr_hi_ready")
        xr_lo_ready = sem("xr_lo_ready")
        kt_ready = sem("kt_ready")
        kt_relued = sem("kt_relued")
        ka_ready = sem("ka_ready")
        ka_hi_ready = sem("ka_hi_ready")
        ka_lo_ready = sem("ka_lo_ready")
        r_ready = sem("r_ready")
        th_ready = sem("th_ready")
        vv_ready = sem("vv_ready")
        y_ready = sem("y_ready")
        out_ready = sem("out_ready")

        def after(eng, s, value):
            if not isinstance(value, int) or value > 0:
                eng.wait_ge(s, value)

        def on(b):
            return not isinstance(b, int) or 0 <= b < NB

        def by_tile(o, u):
            return o[:, :, P * u:P * u + P].rearrange("p k (g a) -> p k g a", g=2 * GR)

        def pipeline(eng, iteration):
            for i in range(-1, 4):
                iteration(i, i % 2)
            with eng.Fori(6, NB // 2 + 3) as pair:
                iteration(pair * 2 - 8, 0)
                iteration(pair * 2 - 7, 1)
            for i in range(NB - 2, NB + 2):
                iteration(i, i % 2)

        block = es.enter_context(nc.Block())

        @block.sync
        def _(sp):
            sp.dma_start(mu_sb[:, 0, :], mu[0]).then_inc(setup_loaded, 16)
            sp.dma_start(mu_sb[:, 1, :], mu[1]).then_inc(setup_loaded, 16)
            sp.dma_start(gates[:, 0:1], g_xattn.rearrange("(a n) -> a n", a=1).broadcast_to([P, 1])).then_inc(setup_loaded, 16)
            sp.dma_start(gates[:, 1:2], g_ffn.rearrange("(a n) -> a n", a=1).broadcast_to([P, 1])).then_inc(setup_loaded, 16)
            sp.dma_start(b_raw, bias.rearrange("(a n) -> a n", a=1)).then_inc(setup_loaded, 16)
            for n in range(4):
                after(sp, setup_dve, 2 + n if n else 0)
                sp.dma_start(w_raw.rearrange("p (c n) -> p c n", c=KC),
                             w_t[n].rearrange("(c p) n -> p c n", p=P)).then_inc(w_loaded, 16)
            sp.wait_ge(setup_dve, 1)
            sp.dma_start(b_rows[1:2, :].bitcast(F32), b_low.bitcast(F32)).then_inc(b_low_moved, 16)

            def load_x(b):
                if on(b):
                    after(sp, q_lo_ready, 2 * b)
                    after(sp, q_hi_ready, 2 * b)
                    for m in range(GR):
                        part = slice(P // 2 * (m % 2), P // 2 * (m % 2) + P // 2)
                        sp.dma_start(x_ln[part, m // 2, :],
                                     x[b].rearrange("(a k m) d -> m k a d", k=KC, m=GR)[m]).then_inc(x_loaded, 16)

            def load_v(b, par):
                if on(b):
                    after(sp, pv_ready, CH * (b - 1))
                    sp.dma_start(v_pos[:, par, :, :], ctx_in[b].rearrange("(v p) d -> p v d", p=P)).then_inc(v_loaded[par], 16)

            def load_k(b, c):
                if on(b):
                    after(sp, k_hi_ready, CH * b + c)
                    after(sp, k_lo_ready, CH * b + c)
                    for r in range(3):
                        sp.dma_start(k_raw[HD * r:HD * r + HD, :, :],
                                     ctx_t[b][:, GR * c:GR * c + GR, :]).then_inc(k_loaded, 16)

            def move_m(b, c):
                if on(b):
                    sp.wait_ge(m_copied, CH * b + c + 1)
                    for piece in range(2):
                        sp.dma_start(q_st[QK + piece:QK + piece + 1, c, :, :].bitcast(F32),
                                     m_t[GR * piece:GR * piece + GR, :].bitcast(F32)).then_inc(m_moved[c % 2], 16)

            def write_o(b, c):
                if on(b):
                    sp.wait_ge(o_ready, CH * b + c + 1)
                    sp.dma_start(o_dram[c].rearrange("g f m r -> (g f) (m r)"), o_val[:, :]).then_inc(o_written, 16)

            def read_o(b, u):
                if on(b):
                    sp.wait_ge(o_written, 16 * (CH * b + 2 * u + 2))
                    for m in range(GR):
                        sp.dma_start(o_mv[HD * m:HD * m + HD, :, :],
                                     o_dram[2 * u:2 * u + 2, :, :, m, :].rearrange("c g f r -> f (c g) r")
                                     ).then_inc(o_moved, 16)

            def store(b, par):
                if on(b):
                    sp.wait_ge(out_ready, NU * (b + 1))
                    sp.dma_start(out[b].rearrange("(u p) d -> p u d", p=P), x1[:, par, :, :]).then_inc(stored, 16)

            def iteration(i, par):
                if isinstance(i, int) and i == -1:
                    load_x(0)
                for s in range(STEPS):
                    if s == 0:
                        load_k(i, 3)
                    if s % 4 == 2:
                        c = (s + 2) // 4 + 0
                        move_m(i if c < CH else i + 1, c % CH)
                    if s == 3:
                        load_v(i + 1, 1 - par)
                    c = s // 4
                    if s % 4 == 2:
                        write_o(i if c >= 1 else i - 1, (c - 1) % CH)
                    if s == 3:
                        read_o(i - 1, 1)
                    if s == 11:
                        read_o(i, 0)
                    if s == 4:
                        load_k(i + 1, 0)
                    if s == 8:
                        load_x(i + 2)
                        load_k(i + 1, 1)
                    if s == 12:
                        load_k(i + 1, 2)
                    if s == 15:
                        store(i - 2, par)

            pipeline(sp, iteration)
            sp.wait_ge(stored, 16 * NB)

        @block.gpsimd
        def _(pool):
            nc.gpsimd.memset(ident_raw, 0.0).then_inc(setup_pool, 1)
            pool.wait_ge(setup_pool, 1)
            nc.gpsimd.affine_select(out=ident_raw, in_=ident_raw, compare_op=ALU.not_equal, fill=1.0,
                                    base=0, pattern=[[-1, P]], channel_multiplier=1).then_inc(setup_pool, 1)
            pool.wait_ge(setup_ones, 1)

            def rstd_1(b):
                if on(b):
                    pool.wait_ge(var_ready, b + 1)
                    after(pool, x_normed, NU * b)
                    nc.gpsimd.tensor_tensor(rstd[:, 0, :], ve[:, 0, :], mhalf[:, 0:1].broadcast_to([P, NU]),
                                            ALU.pow).then_inc(rstd_ready, 1)

            def rstd_2(b, u):
                if on(b):
                    pool.wait_ge(var2_ready, NU * b + u + 1)
                    after(pool, xn_ready, NU * (b - 1) + u + 1)
                    nc.gpsimd.tensor_tensor(rstd[:, 1, u:u + 1], ve[:, 1, u:u + 1], mhalf[:, 0:1],
                                            ALU.pow).then_inc(rstd2_ready, 1)

            def k_low(b, c, *before):
                if on(b):
                    for s, count in before:
                        after(pool, s, count)
                    pool.wait_ge(k_pos, CH * b + c + 1)
                    pool.wait_ge(k_hi_ready, CH * b + c + 1)
                    rows = slice(2 * HD, 3 * HD)
                    nc.gpsimd.tensor_tensor(k_st[rows, c, :, :], k_raw[rows, :, :], k_st[rows, c, :, :].bitcast(F32),
                                            ALU.subtract).then_inc(k_lo_ready, 1)
                    pool.wait_ge(k_lo_ready, CH * b + c + 1)

            def o_low(b, u):
                if on(b):
                    pool.wait_ge(o_hi_ready, NU * b + u + 1)
                    after(pool, z_ready, NU * (b - 1) + u + 1)
                    nc.gpsimd.tensor_tensor(by_tile(o_lo, u), o_mv[:, :, :].rearrange("p g (k a) -> p k g a", k=KC),
                                            by_tile(o_hi, u).bitcast(F32), ALU.subtract).then_inc(o_lo_ready, 1)

            def x_diff(b):
                if on(b):
                    pool.wait_ge(xt_ready, NU * (b + 1))
                    after(pool, xr_hi_ready, b)
                    after(pool, xr_lo_ready, b)
                    nc.gpsimd.tensor_tensor(xd[:, :, :], xt[:, :, 1:T + 1], xt[:, :, 0:T],
                                            ALU.subtract).then_inc(xd_ready, 1)

            def xk_low(b):
                if on(b):
                    pool.wait_ge(xk_ready, b + 1)
                    pool.wait_ge(xk_hi_ready, b + 1)
                    after(pool, kt_ready, 2 * b)
                    nc.gpsimd.tensor_tensor(xk_lo[:, :, :], xm[:, :, :], xk_hi[:, :, :].bitcast(F32),
                                            ALU.subtract).then_inc(xk_lo_ready, 1)

            def xr_low(b):
                if on(b):
                    pool.wait_ge(xr_ready, b + 1)
                    pool.wait_ge(xr_hi_ready, b + 1)
                    after(pool, r_ready, NU * b)
                    nc.gpsimd.tensor_tensor(xr_lo[:, :, :], xd[:, :, :], xr_hi[:, :, :].bitcast(F32),
                                            ALU.subtract).then_inc(xr_lo_ready, 1)

            def ka_square(b, half):
                if on(b):
                    pool.wait_ge(kt_relued, 2 * b + half + 1)
                    part = xm[:, 2 * half:2 * half + 2, :]
                    nc.gpsimd.tensor_tensor(part, part, part, ALU.mult).then_inc(ka_ready, 1)

            def ka_low(b, half):
                if on(b):
                    pool.wait_ge(ka_ready, 2 * b + half + 1)
                    pool.wait_ge(ka_hi_ready, 2 * b + half + 1)
                    after(pool, vv_ready, NU * b)
                    nc.gpsimd.tensor_tensor(ka_lo[:, 2 * half:2 * half + 2, :], xm[:, 2 * half:2 * half + 2, :],
                                            ka_hi[:, 2 * half:2 * half + 2, :].bitcast(F32),
                                            ALU.subtract).then_inc(ka_lo_ready, 1)

            def iteration(i, par):
                for s in range(STEPS):
                    if s == 0:
                        ka_square(i - 2, 0)
                    if s == 1:
                        ka_low(i - 2, 0)
                        k_low(i, 3, (ka_lo_ready, 2 * (i - 2) + 1), (xr_lo_ready, i - 1))
                    if s == 2:
                        ka_square(i - 2, 1)
                    if s == 3:
                        rstd_1(i + 1)
                    if s == 4:
                        ka_low(i - 2, 1)
                    if s == 5:
                        o_low(i - 1, 1)
                    if s == 6:
                        rstd_2(i - 1, 0)
                        k_low(i + 1, 0, (rstd2_ready, NU * (i - 1) + 1), (o_lo_ready, NU * i), (rstd_ready, i + 2))
                    if s == 8:
                        rstd_2(i - 1, 1)
                    if s == 10:
                        k_low(i + 1, 1, (rstd2_ready, NU * (i - 1) + 2))
                    if s == 11:
                        x_diff(i - 1)
                    if s == 13:
                        o_low(i, 0)
                        xk_low(i - 1)
                    if s == 14:
                        k_low(i + 1, 2, (xk_lo_ready, i), (o_lo_ready, NU * i + 1))
                    if s == 15:
                        xr_low(i - 1)

            pipeline(pool, iteration)

        @block.scalar
        def _(act):
            act.wait_ge(setup_loaded, 80)
            nc.scalar.activation(tg[:, :], gates[:, :], ACT.Tanh).then_inc(setup_act, 1)
            act.wait_ge(setup_pool, 2)
            act.wait_ge(setup_ones, 1)
            nc.scalar.activation(ident_r[:, :], ident_raw, ACT.Copy).then_inc(setup_act, 1)
            nc.scalar.activation(b_rows[0:1, :], b_raw, ACT.Copy).then_inc(setup_act, 1)
            for n in range(4):
                act.wait_ge(w_loaded, 16 * (n + 1))
                nc.scalar.activation(w_hi[n][:, :, :].rearrange("p c n -> p (c n)"), w_raw,
                                     ACT.Copy).then_inc(setup_act, 1)
            act.wait_ge(setup_dve, 6)
            act.wait_ge(b_low_moved, 16)

            def load_x1(b, par):
                if on(b):
                    after(act, stored, 16 * (b - 1))
                    act.dma_start(x1[:, par, :, :], x[b].rearrange("(u p) d -> p u d", p=P)).then_inc(x1_loaded, 16)

            def q_high(b, u):
                if on(b):
                    act.wait_ge(x_normed, NU * b + u + 1)
                    after(act, q_turned, 2 * CH * b)
                    xu = x_ln[:, u, :].rearrange("p (h f) -> p h f", h=HEADS)
                    nc.scalar.activation(q_nat[:, u, :, 0, :], xu, ACT.Relu)
                    nc.scalar.activation(q_nat[:, u, :, 2, :], xu, ACT.Relu).then_inc(q_hi_ready, 1)

            def q_stack(b, c, u):
                if on(b):
                    act.wait_ge(q_turned, 2 * CH * b + 2 * c + u + 1)
                    after(act, st_ready, HEADS * (b - 1) + GR * c + GR)
                    nc.scalar.activation(q_st[0:QK, c, :, P * u:P * u + P],
                                         tp_bank[0:QK, :].rearrange("p (g t) -> p g t", g=GR),
                                         ACT.Copy).then_inc(q_stacked, 1)

            def k_high(b, c):
                if on(b):
                    act.wait_ge(k_loaded, 48 * (CH * b + c + 1))
                    after(act, st_ready, HEADS * (b - 1) + GR * c + GR)
                    nc.scalar.activation(k_st[0:QK, c, :, :], k_raw[0:QK, :, :], ACT.Relu).then_inc(k_hi_ready, 1)
                    rows = slice(2 * HD, 3 * HD)
                    act.wait_ge(k_hi_ready, CH * b + c + 1)
                    nc.scalar.activation(k_raw[rows, :, :], k_raw[rows, :, :], ACT.Relu).then_inc(k_pos, 1)

            def exponent(b, n):
                if on(b):
                    act.wait_ge(st_ready, HEADS * b + n + 1)
                    if n % GR == 0:
                        after(act, pv_ready, CH * b + n // GR - 1)
                    nc.scalar.activation(probs[:, n // GR % 2, n % GR, :, :].rearrange("p v t -> p (v t)"),
                                         st_bank[n % 2][:, :], ACT.Exp, scale=SCALE).then_inc(exp_ready, 1)

            def o_high(b, u):
                if on(b):
                    act.wait_ge(o_moved, 16 * GR * (NU * b + u + 1))
                    after(act, z_ready, NU * (b - 1) + u + 1)
                    nc.scalar.activation(by_tile(o_hi, u), o_mv[:, :, :].rearrange("p g (k a) -> p k g a", k=KC),
                                         ACT.Copy).then_inc(o_hi_ready, 1)

            def z_relu(b, u):
                if on(b):
                    act.wait_ge(z_ready, NU * b + u + 1)
                    after(act, xn_turned, NU * (b - 1) + u + 1)
                    nc.scalar.activation(xn[:, u, :], dense_bank[u][:, :], ACT.Relu).then_inc(z_relued, 1)

            def xt_copy(b, u):
                if on(b):
                    act.wait_ge(xn_turned, NU * b + u + 1)
                    after(act, xr_ready, b)
                    nc.scalar.activation(xt[:, :, 1 + P * u:1 + P * u + P],
                                         tp_bank[:, :].rearrange("p (c t) -> p c t", c=KC),
                                         ACT.Copy).then_inc(xt_ready, 1)

            def xk_high(b):
                if on(b):
                    act.wait_ge(xk_ready, b + 1)
                    after(act, kt_ready, 2 * b)
                    nc.scalar.activation(xk_hi[:, :, :], xm[:, :, :], ACT.Copy).then_inc(xk_hi_ready, 1)

            def xr_high(b):
                if on(b):
                    act.wait_ge(xr_ready, b + 1)
                    after(act, r_ready, NU * b)
                    nc.scalar.activation(xr_hi[:, :, :], xd[:, :, :], ACT.Copy).then_inc(xr_hi_ready, 1)

            def kt_relu(b, half):
                if on(b):
                    act.wait_ge(kt_ready, 2 * b + half + 1)
                    act.wait_ge(xk_lo_ready, b + 1)
                    nc.scalar.activation(xm[:, 2 * half:2 * half + 2, :].rearrange("p c t -> p (c t)"),
                                         dense_bank[1 - half][:, :], ACT.Relu).then_inc(kt_relued, 1)

            def ka_high(b, half):
                if on(b):
                    act.wait_ge(ka_ready, 2 * b + half + 1)
                    after(act, vv_ready, NU * b)
                    nc.scalar.activation(ka_hi[:, 2 * half:2 * half + 2, :], xm[:, 2 * half:2 * half + 2, :],
                                         ACT.Copy).then_inc(ka_hi_ready, 1)

            def r_tanh(b, u):
                if on(b):
                    act.wait_ge(r_ready, NU * b + u + 1)
                    after(act, out_ready, NU * (b - 1) + u + 1)
                    nc.scalar.activation(th[:, u, :], dense_bank[1 - u][:, :], ACT.Tanh,
                                         scale=0.5).then_inc(th_ready, 1)

            def iteration(i, par):
                for s in range(STEPS):
                    if s == 0:
                        kt_relu(i - 2, 0)
                    exponent(i, s)
                    if s == 0:
                        q_stack(i, 2, 0)
                        q_stack(i, 2, 1)
                    if s == 1:
                        ka_high(i - 2, 0)
                        q_stack(i, 3, 0)
                        q_stack(i, 3, 1)
                        k_high(i, 3)
                    if s == 2:
                        kt_relu(i - 2, 1)
                        load_x1(i - 1, 1 - par)
                    if s == 3:
                        ka_high(i - 2, 1)
                    if s == 4:
                        r_tanh(i - 2, 0)
                        q_high(i + 1, 0)
                    if s == 5:
                        o_high(i - 1, 1)
                        q_high(i + 1, 1)
                        k_high(i + 1, 0)
                    if s == 6:
                        z_relu(i - 1, 0)
                    if s == 8:
                        z_relu(i - 1, 1)
                        q_stack(i + 1, 0, 0)
                        q_stack(i + 1, 0, 1)
                    if s == 9:
                        xt_copy(i - 1, 0)
                        k_high(i + 1, 1)
                    if s == 10:
                        r_tanh(i - 2, 1)
                        xt_copy(i - 1, 1)
                    if s == 12:
                        q_stack(i + 1, 1, 0)
                        q_stack(i + 1, 1, 1)
                    if s == 13:
                        o_high(i, 0)
                        xk_high(i - 1)
                        k_high(i + 1, 2)
                    if s == 15:
                        xr_high(i - 1)

            pipeline(act, iteration)

        @block.vector
        def _(dve):
            nc.vector.memset(b_rows[:, :].bitcast(F32), 0.0)
            nc.vector.memset(ones_r[:, :].bitcast(F32), 1.0)
            nc.vector.memset(mhalf[:, :], -0.5)
            nc.vector.memset(xt[:, :, 0:1], 0.0)
            nc.vector.memset(k_st[QK:P, :, :, :].bitcast(F32), 1.0).then_inc(setup_ones, 1)
            dve.wait_ge(setup_act, 3)
            nc.vector.tensor_tensor(b_low, b_raw, b_rows[0:1, :].bitcast(F32), ALU.subtract).then_inc(setup_dve, 1)
            nc.vector.tensor_scalar(tgh[:, :], tg[:, 1:2], 0.5, None, ALU.mult).then_inc(setup_dve, 1)
            for n in range(4):
                dve.wait_ge(setup_act, 4 + n)
                nc.vector.tensor_tensor(w_lo[n][:, :, :].rearrange("p c n -> p (c n)"), w_raw,
                                        w_hi[n][:, :, :].rearrange("p c n -> p (c n)").bitcast(F32),
                                        ALU.subtract).then_inc(setup_dve, 1)
            dve.wait_ge(setup_dve, 6)

            def stats_1(b):
                if on(b):
                    dve.wait_ge(x_loaded, 16 * GR * (b + 1))
                    for u in range(NU):
                        last = nc.vector.bn_stats(st6[:, 0, u, :], x_ln[:, u, :])
                    last.then_inc(stat1, 1)
                    dve.wait_ge(stat1, b + 1)
                    nc.vector.memset(carrier[:, :], 0.0)
                    for u in range(NU):
                        last = nc.vector.bn_aggr(mv[:, 0, u, :], st6[:, 0, u, :])
                    last.then_inc(mv1, 1)
                    dve.wait_ge(mv1, b + 1)
                    after(dve, rstd_ready, b)
                    nc.vector.tensor_scalar(ve[:, 0, :], mv[:, 0, :, 1], LN_EPS, None, ALU.add).then_inc(var_ready, 1)

            def norm_1(b):
                if on(b):
                    dve.wait_ge(rstd_ready, b + 1)
                    for u in range(NU):
                        nc.vector.tensor_scalar(x_ln[:, u, :], x_ln[:, u, :], mv[:, 0, u, 0:1], rstd[:, 0, u:u + 1],
                                                ALU.subtract, ALU.mult).then_inc(x_normed, 1)

            def q_low(b, u):
                if on(b):
                    dve.wait_ge(q_hi_ready, NU * b + u + 1)
                    nc.vector.scalar_tensor_tensor(out=q_nat[:, u, :, 1, :],
                                                   in0=x_ln[:, u, :].rearrange("p (h f) -> p h f", h=HEADS), scalar=0.0,
                                                   in1=q_nat[:, u, :, 0, :].bitcast(F32), op0=ALU.max,
                                                   op1=ALU.subtract).then_inc(q_lo_ready, 1)

            def relu_v(b, par):
                if on(b):
                    dve.wait_ge(v_loaded[par], 8 * (b - par) + 16)
                    part = v_pos[:, par, :, :]
                    nc.vector.tensor_scalar(part, part, 0.0, None, ALU.max).then_inc(v_ready, 1)

            def head_max(b, n):
                if on(b):
                    dve.wait_ge(s_ready, HEADS * b + n + 1)
                    if n % GR == 0:
                        after(dve, m_split, CH * b + n // GR)
                    nc.vector.tensor_reduce(nmax[:, :, n % GR:n % GR + 1],
                                            s_bank[n % 2][:, :].rearrange("p (u y) -> p u y", u=NU),
                                            AX_X, ALU.max, negate=True).then_inc(s_maxed, 1)

            def split_m(b, c):
                if on(b):
                    dve.wait_ge(s_maxed, HEADS * b + GR * c + GR)
                    after(dve, m_turned, CH * b + c)
                    nc.vector.tensor_copy(m_nat[:, :, 0, :], nmax[:, :, :]).then_inc(m_hi_ready, 1)
                    dve.wait_ge(m_hi_ready, CH * b + c + 1)
                    nc.vector.tensor_tensor(m_nat[:, :, 1, :], nmax[:, :, :], m_nat[:, :, 0, :].bitcast(F32),
                                            ALU.subtract).then_inc(m_split, 1)

            def copy_m(b, c):
                if on(b):
                    dve.wait_ge(m_turned, CH * b + c + 1)
                    after(dve, m_moved[(c + 1) % 2], 32 * (2 * b + (c + 1) // 2))
                    nc.vector.tensor_copy(m_t[0:2 * GR, :], tp_bank[0:2 * GR, 0:T]).then_inc(m_copied, 1)

            def norm_o(b, c):
                if on(b):
                    dve.wait_ge(pv_ready, CH * b + c + 1)
                    after(dve, o_written, 16 * (CH * b + c))
                    if c % 2 == 1:
                        after(dve, o_lo_ready, NU * b + c // 2)
                    nc.vector.reciprocal(o_val[:, :], pv_bank[:, T:2 * T]).then_inc(rden_ready, 1)
                    dve.wait_ge(rden_ready, CH * b + c + 1)
                    nc.vector.tensor_tensor(o_val[:, :], pv_bank[:, 0:T], o_val[:, :],
                                            ALU.mult).then_inc(o_ready, 1)

            def add_x(b, u, par):
                if on(b):
                    dve.wait_ge(z_relued, NU * b + u + 1)
                    dve.wait_ge(x1_loaded, 16 * (b + 1))
                    nc.vector.scalar_tensor_tensor(out=x1[:, par, u, :], in0=xn[:, u, :], scalar=tg[:, 0:1],
                                                   in1=x1[:, par, u, :], op0=ALU.mult, op1=ALU.add).then_inc(x1_ready, 1)
                    dve.wait_ge(x1_ready, NU * b + u + 1)
                    nc.vector.bn_stats(st6[:, 1, u, :], x1[:, par, u, :]).then_inc(stat2, 1)
                    dve.wait_ge(stat2, NU * b + u + 1)
                    nc.vector.memset(carrier[:, :], 0.0)
                    nc.vector.bn_aggr(mv[:, 1, u, :], st6[:, 1, u, :]).then_inc(mv2, 1)
                    dve.wait_ge(mv2, NU * b + u + 1)
                    after(dve, rstd2_ready, NU * (b - 1) + u + 1)
                    nc.vector.tensor_scalar(ve[:, 1, u:u + 1], mv[:, 1, u, 1:2], LN_EPS, None,
                                            ALU.add).then_inc(var2_ready, 1)

            def norm_2(b, u, par):
                if on(b):
                    dve.wait_ge(rstd2_ready, NU * b + u + 1)
                    nc.vector.tensor_scalar(xn[:, u, :], x1[:, par, u, :], mv[:, 1, u, 0:1], rstd[:, 1, u:u + 1],
                                            ALU.subtract, ALU.mult).then_inc(xn_ready, 1)

            def mix_k(b):
                if on(b):
                    dve.wait_ge(xd_ready, b + 1)
                    after(dve, ka_lo_ready, 2 * b)
                    for c in range(KC):
                        last = nc.vector.scalar_tensor_tensor(out=xm[:, c, :], in0=xd[:, c, :], scalar=mu_sb[:, 1, c:c + 1],
                                                              in1=xt[:, c, 0:T], op0=ALU.mult, op1=ALU.add)
                    last.then_inc(xk_ready, 1)

            def mix_r(b):
                if on(b):
                    dve.wait_ge(xk_ready, b + 1)
                    for c in range(KC):
                        last = nc.vector.scalar_tensor_tensor(out=xd[:, c, :], in0=xd[:, c, :], scalar=mu_sb[:, 0, c:c + 1],
                                                              in1=xt[:, c, 0:T], op0=ALU.mult, op1=ALU.add)
                    last.then_inc(xr_ready, 1)

            def finish(b, u, par):
                if on(b):
                    dve.wait_ge(vv_ready, NU * b + u + 1)
                    dve.wait_ge(th_ready, NU * b + u + 1)
                    nc.vector.scalar_tensor_tensor(out=th[:, u, :], in0=th[:, u, :], scalar=1.0,
                                                   in1=dense_bank[1 - u][:, :], op0=ALU.add, op1=ALU.mult).then_inc(y_ready, 1)
                    dve.wait_ge(y_ready, NU * b + u + 1)
                    nc.vector.scalar_tensor_tensor(out=x1[:, par, u, :], in0=th[:, u, :], scalar=tgh[:, 0:1],
                                                   in1=x1[:, par, u, :], op0=ALU.mult, op1=ALU.add).then_inc(out_ready, 1)

            def iteration(i, par):
                for s in range(STEPS):
                    c = s // 4
                    if s % 4 == 2:
                        copy_m(i if c + 1 < CH else i + 1, (c + 1) % CH)
                    n = s + AHEAD
                    head_max(i if n < HEADS else i + 1, n % HEADS)
                    if s % 4 == 1:
                        split_m(i if c + 1 < CH else i + 1, (c + 1) % CH)
                    if s % 4 == 2:
                        norm_o(i if c >= 1 else i - 1, (c - 1) % CH)
                    if s == 2:
                        stats_1(i + 1)
                    if s == 3:
                        norm_1(i + 1)
                    if s == 5:
                        q_low(i + 1, 0)
                    if s == 6:
                        q_low(i + 1, 1)
                        add_x(i - 1, 0, 1 - par)
                    if s == 7:
                        norm_2(i - 1, 0, 1 - par)
                    if s == 8:
                        add_x(i - 1, 1, 1 - par)
                        norm_2(i - 1, 1, 1 - par)
                    if s == 12:
                        mix_k(i - 1)
                        finish(i - 2, 0, par)
                    if s == 13:
                        relu_v(i + 1, 1 - par)
                    if s == 14:
                        mix_r(i - 1)
                        finish(i - 2, 1, par)

            pipeline(dve, iteration)

        @block.tensor
        def _(pe):
            pe.wait_ge(setup_act, 7)
            pe.wait_ge(setup_dve, 6)
            pe.wait_ge(setup_pool, 2)
            pe.wait_ge(setup_ones, 1)
            pe.wait_ge(b_low_moved, 16)

            def freed(i, *copies):
                for s, b, per, k in copies if isinstance(i, int) else copies[:1]:
                    value = b * per + k
                    if isinstance(value, int):
                        value = min(value, NB * per)
                    after(pe, s, value)

            def turn_q(b, c, u, i, *users):
                if on(b):
                    pe.wait_ge(q_hi_ready, NU * b + u + 1)
                    pe.wait_ge(q_lo_ready, NU * b + u + 1)
                    freed(i, *users)
                    for g in range(GR):
                        mm = nc.tensor.transpose(tp_bank[0:QK, P * g:P * g + P].bitcast(F32R),
                                                 q_nat[:, u, GR * c + g, :, :], ident_r[:, :])
                    mm.then_inc(q_turned, 1)

            def turn_m(b, c, i, *users):
                if on(b):
                    pe.wait_ge(m_split, CH * b + c + 1)
                    freed(i, *users)
                    for u in range(NU):
                        mm = nc.tensor.transpose(tp_bank[0:2 * GR, P * u:P * u + P].bitcast(F32R),
                                                 m_nat[:, u, :, :], ident_r[:, :])
                    mm.then_inc(m_turned, 1)

            def turn_xn(b, u, i, *users):
                if on(b):
                    pe.wait_ge(xn_ready, NU * b + u + 1)
                    freed(i, *users)
                    for c in range(KC):
                        mm = nc.tensor.transpose(tp_bank[:, P * c:P * c + P], xn[:, u, P * c:P * c + P],
                                                 ident_r[:, :].bitcast(F32))
                    mm.then_inc(xn_turned, 1)

            def scores(b, n):
                if on(b):
                    c, g = n // GR, n % GR
                    if g == 0:
                        pe.wait_ge(q_stacked, 2 * CH * b + 2 * c + 2)
                        pe.wait_ge(k_hi_ready, CH * b + c + 1)
                        pe.wait_ge(k_lo_ready, CH * b + c + 1)
                    after(pe, s_maxed, HEADS * b + n - 1)
                    for u in range(NU):
                        mm = nc.tensor.matmul(s_bank[n % 2][:, T * u:T * u + T], q_st[0:QK, c, g, P * u:P * u + P],
                                              k_st[0:QK, c, g, :], start=True, stop=True)
                    mm.then_inc(s_ready, 1)

            def shifted_scores(b, n):
                if on(b):
                    c, g = n // GR, n % GR
                    if g == 0:
                        pe.wait_ge(m_moved[c % 2], 32 * (2 * b + c // 2 + 1))
                    after(pe, exp_ready, HEADS * b + n - 1)
                    for v in range(NU):
                        mm = nc.tensor.matmul(st_bank[n % 2][:, T * v:T * v + T], k_st[0:ST, c, g, P * v:P * v + P],
                                              q_st[0:ST, c, g, :], start=True, stop=True)
                    mm.then_inc(st_ready, 1)

            def values(b, c, par):
                if on(b):
                    pe.wait_ge(exp_ready, HEADS * b + GR * c + GR)
                    pe.wait_ge(v_ready, b + 1)
                    after(pe, o_ready, CH * b + c)
                    for v in range(NU):
                        for g in range(GR):
                            h = GR * c + g
                            nc.tensor.matmul(pv_bank[HD * g:HD * g + HD, 0:T], v_pos[:, par, v, HD * h:HD * h + HD],
                                             probs[:, c % 2, g, v, :], start=(v == 0), stop=(v == NU - 1))
                    for v in range(NU):
                        for g in range(GR):
                            mm = nc.tensor.matmul(pv_bank[HD * g:HD * g + HD, T:2 * T], ones_r[:, 0:HD].bitcast(F32),
                                                  probs[:, c % 2, g, v, :], start=(v == 0), stop=(v == NU - 1))
                    mm.then_inc(pv_ready, 1)

            def product(dst, lhs, rhs, first, last):
                for n, (a, c) in enumerate(((0, 0), (1, 0), (0, 1))):
                    mm = nc.tensor.matmul(dst, lhs[a], rhs[c], start=first and n == 0, stop=last and n == 2)
                return mm

            def project(b, u, part, i, *users):
                if on(b):
                    if part == 0:
                        freed(i, *users)
                        nc.tensor.matmul(dense_bank[u][:, :], ones_r[:, :], b_rows[:, :], start=True, stop=False)
                        pe.wait_ge(o_hi_ready, NU * b + u + 1)
                        pe.wait_ge(o_lo_ready, NU * b + u + 1)
                    rows = slice(P * u, P * u + P)
                    mm = product(dense_bank[u][:, :], (o_hi[:, part, rows], o_lo[:, part, rows]),
                                 (w_hi[W_X][:, part, :], w_lo[W_X][:, part, :]), False, part == KC - 1)
                    if part == KC - 1:
                        mm.then_inc(z_ready, 1)

            def receptance(b, u, part, i, *users):
                if on(b):
                    if part == 0:
                        freed(i, *users)
                        pe.wait_ge(xr_hi_ready, b + 1)
                        pe.wait_ge(xr_lo_ready, b + 1)
                    rows = slice(P * u, P * u + P)
                    mm = product(dense_bank[1 - u][:, :], (xr_hi[:, part, rows], xr_lo[:, part, rows]),
                                 (w_hi[W_R][:, part, :], w_lo[W_R][:, part, :]), part == 0, part == KC - 1)
                    if part == KC - 1:
                        mm.then_inc(r_ready, 1)

            def key(b, half, part, i, *users):
                if on(b):
                    if part == 0:
                        freed(i, *users)
                        pe.wait_ge(xk_hi_ready, b + 1)
                        pe.wait_ge(xk_lo_ready, b + 1)
                    m = part // 2
                    n = 2 * half + m
                    cols = slice(P * n, P * n + P)
                    for kc in (2 * (part % 2), 2 * (part % 2) + 1):
                        mm = product(dense_bank[1 - half][:, T * m:T * m + T],
                                     (w_hi[W_K][:, kc, cols], w_lo[W_K][:, kc, cols]),
                                     (xk_hi[:, kc, :], xk_lo[:, kc, :]), kc == 0, kc == KC - 1)
                    if part == 3:
                        mm.then_inc(kt_ready, 1)

            def value(b, u, part, i, *users):
                if on(b):
                    if part == 0:
                        freed(i, *users)
                    if part % 2 == 0:
                        pe.wait_ge(ka_hi_ready, 2 * b + part // 2 + 1)
                        pe.wait_ge(ka_lo_ready, 2 * b + part // 2 + 1)
                    rows = slice(P * u, P * u + P)
                    mm = product(dense_bank[1 - u][:, :], (ka_hi[:, part, rows], ka_lo[:, part, rows]),
                                 (w_hi[W_V][:, part, :], w_lo[W_V][:, part, :]), part == 0, part == KC - 1)
                    if part == KC - 1:
                        mm.then_inc(vv_ready, 1)

            def iteration(i, par):
                def stacked(b, c, u):
                    return q_stacked, b, 2 * CH, 2 * c + u + 1

                def copied(b, c):
                    return m_copied, b, CH, c + 1

                def xt_done(b, u):
                    return xt_ready, b, NU, u + 1

                def dense(q, part):
                    b1, b2 = i - 1, i - 2
                    if q == 0:
                        key(b2, 1, part, i, (y_ready, i - 3, NU, 2), (th_ready, i - 3, NU, 2), (z_relued, b2, NU, 1))
                    if q == 1:
                        receptance(b2, 0, part, i, (kt_relued, b2, 2, 1))
                    if q == 2:
                        project(b1, 0, part, i, (kt_relued, b2, 2, 2))
                    if q == 3:
                        project(b1, 1, part, i, (th_ready, b2, NU, 1))
                    if q == 4:
                        receptance(b2, 1, part, i, (z_relued, b1, NU, 1), (kt_relued, b2, 2, 2))
                    if q == 5:
                        value(b2, 0, part, i, (z_relued, b1, NU, 2), (th_ready, b2, NU, 1))
                    if q == 6:
                        value(b2, 1, part, i, (th_ready, b2, NU, 2))
                    if q == 7:
                        key(b1, 0, part, i, (y_ready, b2, NU, 1), (z_relued, b1, NU, 2))

                for s in range(STEPS):
                    c = s // 4
                    if s == 0:
                        turn_q(i, 2, 0, i, copied(i, 0), stacked(i, 1, 1), xt_done(i - 2, 1))
                    if s == 1:
                        turn_q(i, 3, 0, i, stacked(i, 2, 1), copied(i, 0), xt_done(i - 2, 1))
                    if s == 2:
                        turn_m(i, 1, i, stacked(i, 3, 1), copied(i, 0), xt_done(i - 2, 1))
                    if s == 6:
                        turn_m(i, 2, i, copied(i, 1), stacked(i, 3, 1), xt_done(i - 2, 1))
                    if s == 8:
                        turn_q(i + 1, 0, 0, i, copied(i, 2), stacked(i, 3, 1), xt_done(i - 2, 1))
                    if s == 9:
                        turn_xn(i - 1, 0, i, stacked(i + 1, 0, 1), copied(i, 2), xt_done(i - 2, 1))
                    if s == 10:
                        turn_m(i, 3, i, xt_done(i - 1, 0), stacked(i + 1, 0, 1), copied(i, 2))
                    if s == 12:
                        turn_q(i + 1, 1, 0, i, xt_done(i - 1, 1), stacked(i + 1, 0, 1), copied(i, 3))
                    if s == 14:
                        turn_m(i + 1, 0, i, stacked(i + 1, 1, 1), copied(i, 3), xt_done(i - 1, 1))
                    shifted_scores(i, s)
                    dense(s // 2, 2 * (s % 2))
                    if s == 0:
                        turn_q(i, 2, 1, i, stacked(i, 2, 0), copied(i, 0), xt_done(i - 2, 1))
                    if s == 1:
                        turn_q(i, 3, 1, i, stacked(i, 3, 0), copied(i, 0), xt_done(i - 2, 1))
                    if s == 8:
                        turn_q(i + 1, 0, 1, i, stacked(i + 1, 0, 0), copied(i, 2), xt_done(i - 2, 1))
                    if s == 10:
                        turn_xn(i - 1, 1, i, copied(i, 3), stacked(i + 1, 0, 1), xt_done(i - 1, 0))
                    if s == 12:
                        turn_q(i + 1, 1, 1, i, stacked(i + 1, 1, 0), copied(i, 3), xt_done(i - 1, 1))
                    n = s + AHEAD
                    scores(i if n < HEADS else i + 1, n % HEADS)
                    dense(s // 2, 2 * (s % 2) + 1)
                    if s % 4 == 1:
                        values(i if c >= 1 else i - 1, (c - 1) % CH, par if c >= 1 else 1 - par)

            pipeline(pe, iteration)


def kernel(**inputs):
    import numpy as np
    import concourse.bacc as bacc
    from concourse.bass_utils import run_bass_kernel_spmd

    x = np.asarray(inputs["x"])
    ctx_in = np.asarray(inputs["ctx_1024"])
    nb, t, d = ctx_in.shape
    ctx_t = ctx_in.reshape(nb, t, HEADS, d // HEADS).transpose(0, 3, 2, 1)
    arrays = {
        "x": x,
        "ctx": ctx_in,
        "ctx_t": ctx_t,
        "g_xattn": np.asarray(inputs["g_xattn"]),
        "g_ffn": np.asarray(inputs["g_ffn"]),
        "w_x": np.asarray(inputs["L0_xattn_ffn_w"]).T,
        "w_r": np.asarray(inputs["L0_ffn_W_r"]).T,
        "w_k": np.asarray(inputs["L0_ffn_W_k"]).T,
        "w_v": np.asarray(inputs["L0_ffn_W_v"]).T,
        "bias": np.asarray(inputs["L0_xattn_ffn_b"]),
        "mu_r": np.asarray(inputs["L0_ffn_mu_r"]).reshape(-1, P).T,
        "mu_k": np.asarray(inputs["L0_ffn_mu_k"]).reshape(-1, P).T,
    }
    arrays = {name: np.ascontiguousarray(a) for name, a in arrays.items()}
    nc = bacc.Bacc("TRN2", target_bir_lowering=False, num_devices=1)
    h = {name: nc.dram_tensor(name + "_dram", a.shape, mybir.dt.from_np(a.dtype), kind="ExternalInput").ap()
         for name, a in arrays.items()}
    out = nc.dram_tensor("out_dram", x.shape, mybir.dt.from_np(x.dtype), kind="ExternalOutput").ap()
    flamingo_block(nc, h["x"], h["ctx"], h["ctx_t"], h["g_xattn"], h["g_ffn"],
                   [h["w_x"], h["w_r"], h["w_k"], h["w_v"]], h["bias"], [h["mu_r"], h["mu_k"]], out)
    r = run_bass_kernel_spmd(nc, [{name + "_dram": a for name, a in arrays.items()}], core_ids=[0])
    return r.results[0]["out_dram"]
```

```python
from contextlib import ExitStack

import concourse.bass as bass
from concourse import mybir

F32 = mybir.dt.float32
F32R = mybir.dt.float32r
ALU = mybir.AluOpType
ACT = mybir.ActivationFunctionType
AX_X = mybir.AxisListType.X

P = 128
HEADS = 16
LN_EPS = 1e-5


def flamingo_block(nc, x, ctx_in, ctx_t, g_xattn, g_ffn, w_t, bias, mu, out):
    NB, T, D = x.shape
    HD = D // HEADS
    NU = T // P
    KC = D // P
    GR = P // HD
    CH = HEADS // GR
    STEPS = HEADS
    SCALE = float(HD) ** -0.5
    assert NU == 2 and KC == 4 and GR == 4 and CH == 4 and HD == 32
    QK = 3 * HD
    ST = QK + 2
    AHEAD = 7

    es = ExitStack()
    with es:
        def sb(name, shape, dt=F32):
            return es.enter_context(nc.sbuf_tensor(name, shape, dt))

        def sem(name):
            return es.enter_context(nc.semaphore(name))

        o_dram = nc.dram_tensor("o_dram", [CH, GR, HD, GR, T // GR], F32, kind="Internal").ap()

        w_hi = [sb(f"w_hi{n}", [P, KC, D], F32R) for n in range(4)]
        w_lo = [sb(f"w_lo{n}", [P, KC, D], F32R) for n in range(4)]
        W_X, W_R, W_K, W_V = range(4)
        x_ln = sb("x_ln", [P, NU, D])
        q_nat = sb("q_nat", [P, NU, HEADS, 3, HD], F32R)
        v_pos = sb("v_pos", [P, 2, NU, D])
        k_raw = sb("k_raw", [P, GR, T])
        k_st = sb("k_st", [P, CH, GR, T], F32R)
        q_st = sb("q_st", [P, CH, GR, T], F32R)
        probs = sb("probs", [P, 2, GR, NU, T])
        o_val = sb("o_val", [P, T])
        o_mv = sb("o_mv", [P, 2 * GR, T // GR])
        o_hi = sb("o_hi", [P, KC, T], F32R)
        o_lo = sb("o_lo", [P, KC, T], F32R)
        x1 = sb("x1", [P, 2, NU, D])
        xn = sb("xn", [P, NU, D])
        xt = sb("xt", [P, KC, T + 1])
        xd = sb("xd", [P, KC, T])
        xm = sb("xm", [P, KC, T])
        xr_hi = sb("xr_hi", [P, KC, T], F32R)
        xr_lo = sb("xr_lo", [P, KC, T], F32R)
        xk_hi = sb("xk_hi", [P, KC, T], F32R)
        xk_lo = sb("xk_lo", [P, KC, T], F32R)
        ka_hi = sb("ka_hi", [P, KC, T], F32R)
        ka_lo = sb("ka_lo", [P, KC, T], F32R)
        th = sb("th", [P, NU, D])
        b_rows = sb("b_rows", [P, D], F32R)
        ones_r = sb("ones_r", [P, P], F32R)
        ident_r = sb("ident_r", [P, P], F32R)
        m_t = sb("m_t", [P, T], F32R)
        nmax = sb("nmax", [P, NU, GR])
        m_nat = sb("m_nat", [P, NU, 2, GR], F32R)
        st6 = sb("st6", [P, 2, NU, 6])
        mv = sb("mv", [P, 2, NU, 2])
        ve = sb("ve", [P, 2, NU])
        rstd = sb("rstd", [P, 2, NU])
        carrier = sb("carrier", [P, 1])
        mhalf = sb("mhalf", [P, 1])
        mu_sb = sb("mu_sb", [P, 2, KC])
        gates = sb("gates", [P, 2])
        tg = sb("tg", [P, 2])
        tgh = sb("tgh", [P, 1])
        w_raw = [probs[:, n, :, :, :].rearrange("p g v t -> p (g v t)") for n in range(2)]
        ident_raw = xn[:, 0, 0:P]
        b_raw = th[0:1, 0, :]
        b_low = th[0:1, 1, :].bitcast(F32R)

        bank = [es.enter_context(nc.psum_tensor(f"bank{n}", [P, 512], F32)) for n in range(8)]
        s_bank, st_bank, pv_bank, dense_bank, tp_bank = bank[0:2], bank[2:4], bank[4], bank[5:7], bank[7]

        x_loaded = sem("x_loaded")
        v_loaded = [sem("v_loaded0"), sem("v_loaded1")]
        k_loaded = sem("k_loaded")
        x1_loaded = sem("x1_loaded")
        m_moved = [sem("m_moved0"), sem("m_moved1")]
        stored = sem("stored")
        setup_loaded = sem("setup_loaded")
        w_loaded = [sem("w_loaded0"), sem("w_loaded1")]
        setup_pool = sem("setup_pool")
        setup_ones = sem("setup_ones")
        setup_act = sem("setup_act")
        setup_dve = sem("setup_dve")
        b_low_moved = sem("b_low_moved")
        var_ready = sem("var_ready")
        rstd_ready = sem("rstd_ready")
        x_normed = sem("x_normed")
        q_hi_ready = sem("q_hi_ready")
        q_lo_ready = sem("q_lo_ready")
        q_turned = sem("q_turned")
        q_stacked = sem("q_stacked")
        v_ready = sem("v_ready")
        k_pos = sem("k_pos")
        k_hi_ready = sem("k_hi_ready")
        k_lo_ready = sem("k_lo_ready")
        s_ready = sem("s_ready")
        s_maxed = sem("s_maxed")
        m_hi_ready = sem("m_hi_ready")
        m_split = sem("m_split")
        m_turned = sem("m_turned")
        m_copied = sem("m_copied")
        st_ready = sem("st_ready")
        exp_ready = sem("exp_ready")
        pv_ready = sem("pv_ready")
        rden_ready = sem("rden_ready")
        o_ready = sem("o_ready")
        o_written = sem("o_written")
        o_moved = sem("o_moved")
        o_hi_ready = sem("o_hi_ready")
        o_lo_ready = sem("o_lo_ready")
        z_ready = sem("z_ready")
        z_relued = sem("z_relued")
        x1_ready = sem("x1_ready")
        stat2 = sem("stat2")
        mv2 = sem("mv2")
        stat1 = sem("stat1")
        mv1 = sem("mv1")
        var2_ready = sem("var2_ready")
        rstd2_ready = sem("rstd2_ready")
        xn_ready = sem("xn_ready")
        xn_turned = sem("xn_turned")
        xt_ready = sem("xt_ready")
        xd_ready = sem("xd_ready")
        xk_ready = sem("xk_ready")
        xk_hi_ready = sem("xk_hi_ready")
        xk_lo_ready = sem("xk_lo_ready")
        xr_ready = sem("xr_ready")
        xr_hi_ready = sem("xr_hi_ready")
        xr_lo_ready = sem("xr_lo_ready")
        kt_ready = sem("kt_ready")
        kt_relued = sem("kt_relued")
        ka_ready = sem("ka_ready")
        ka_hi_ready = sem("ka_hi_ready")
        ka_lo_ready = sem("ka_lo_ready")
        r_ready = sem("r_ready")
        th_ready = sem("th_ready")
        vv_ready = sem("vv_ready")
        y_ready = sem("y_ready")
        out_ready = sem("out_ready")

        def after(eng, s, value):
            if not isinstance(value, int) or value > 0:
                eng.wait_ge(s, value)

        def on(b):
            return not isinstance(b, int) or 0 <= b < NB

        def by_tile(o, u):
            return o[:, :, P * u:P * u + P].rearrange("p k (g a) -> p k g a", g=2 * GR)

        def pipeline(eng, iteration):
            for i in range(-1, 4):
                iteration(i, i % 2)
            with eng.Fori(6, NB // 2 + 3) as pair:
                iteration(pair * 2 - 8, 0)
                iteration(pair * 2 - 7, 1)
            for i in range(NB - 2, NB + 3):
                iteration(i, i % 2)

        block = es.enter_context(nc.Block())

        @block.sync
        def _(sp):
            sp.dma_start(mu_sb[:, 0, :], mu[0]).then_inc(setup_loaded, 16)
            sp.dma_start(mu_sb[:, 1, :], mu[1]).then_inc(setup_loaded, 16)
            sp.dma_start(gates[:, 0:1], g_xattn.rearrange("(a n) -> a n", a=1).broadcast_to([P, 1])).then_inc(setup_loaded, 16)
            sp.dma_start(gates[:, 1:2], g_ffn.rearrange("(a n) -> a n", a=1).broadcast_to([P, 1])).then_inc(setup_loaded, 16)
            sp.dma_start(b_raw, bias.rearrange("(a n) -> a n", a=1)).then_inc(setup_loaded, 16)
            for n in range(4):
                after(sp, setup_dve, 1 + n if n > 1 else 0)
                sp.dma_start(w_raw[n % 2].rearrange("p (c n) -> p c n", c=KC),
                             w_t[n].rearrange("(c p) n -> p c n", p=P)).then_inc(w_loaded[n % 2], 16)
            sp.wait_ge(setup_dve, 1)
            sp.dma_start(b_rows[1:2, :].bitcast(F32), b_low.bitcast(F32)).then_inc(b_low_moved, 16)

            def load_x(b):
                if on(b):
                    after(sp, q_lo_ready, 2 * b)
                    after(sp, q_hi_ready, 2 * b)
                    for m in range(GR):
                        part = slice(P // 2 * (m % 2), P // 2 * (m % 2) + P // 2)
                        sp.dma_start(x_ln[part, m // 2, :],
                                     x[b].rearrange("(a k m) d -> m k a d", k=KC, m=GR)[m]).then_inc(x_loaded, 16)

            def load_v(b, par):
                if on(b):
                    after(sp, pv_ready, CH * (b - 1))
                    sp.dma_start(v_pos[:, par, :, :], ctx_in[b].rearrange("(v p) d -> p v d", p=P)).then_inc(v_loaded[par], 16)

            def load_k(b, c):
                if on(b):
                    after(sp, k_hi_ready, CH * b + c)
                    after(sp, k_lo_ready, CH * b + c)
                    for r in range(3):
                        sp.dma_start(k_raw[HD * r:HD * r + HD, :, :],
                                     ctx_t[b][:, GR * c:GR * c + GR, :]).then_inc(k_loaded, 16)

            def move_m(b, c):
                if on(b):
                    sp.wait_ge(m_copied, CH * b + c + 1)
                    for piece in range(2):
                        sp.dma_start(q_st[QK + piece:QK + piece + 1, c, :, :].bitcast(F32),
                                     m_t[GR * piece:GR * piece + GR, :].bitcast(F32)).then_inc(m_moved[c % 2], 16)

            def write_o(b, c):
                if on(b):
                    sp.wait_ge(o_ready, CH * b + c + 1)
                    sp.dma_start(o_dram[c].rearrange("g f m r -> (g f) (m r)"), o_val[:, :]).then_inc(o_written, 16)

            def read_o(b, u):
                if on(b):
                    sp.wait_ge(o_written, 16 * (CH * b + 2 * u + 2))
                    for m in range(GR):
                        sp.dma_start(o_mv[HD * m:HD * m + HD, :, :],
                                     o_dram[2 * u:2 * u + 2, :, :, m, :].rearrange("c g f r -> f (c g) r")
                                     ).then_inc(o_moved, 16)

            def store(b, par):
                if on(b):
                    sp.wait_ge(out_ready, NU * (b + 1))
                    sp.dma_start(out[b].rearrange("(u p) d -> p u d", p=P), x1[:, par, :, :]).then_inc(stored, 16)

            def iteration(i, par):
                if isinstance(i, int) and i == -1:
                    load_x(0)
                for s in range(STEPS):
                    c = s // 4
                    if s == 0:
                        load_k(i, 3)
                    if s == 1:
                        store(i - 3, 1 - par)
                    if s in (1, 5, 9):
                        move_m(i, c + 1)
                    if s == 14:
                        move_m(i + 1, 0)
                    if s % 4 == 1:
                        write_o(i if c >= 1 else i - 1, (c - 1) % CH)
                    if s == 2:
                        read_o(i - 1, 1)
                    if s == 3:
                        load_v(i + 1, 1 - par)
                    if s == 4:
                        load_k(i + 1, 0)
                    if s == 7:
                        load_k(i + 1, 1)
                    if s == 8:
                        load_x(i + 2)
                    if s == 10:
                        read_o(i, 0)
                    if s == 12:
                        load_k(i + 1, 2)

            pipeline(sp, iteration)
            sp.wait_ge(stored, 16 * NB)

        @block.gpsimd
        def _(pool):
            nc.gpsimd.memset(ident_raw, 0.0).then_inc(setup_pool, 1)
            pool.wait_ge(setup_pool, 1)
            nc.gpsimd.affine_select(out=ident_raw, in_=ident_raw, compare_op=ALU.not_equal, fill=1.0,
                                    base=0, pattern=[[-1, P]], channel_multiplier=1).then_inc(setup_pool, 1)
            pool.wait_ge(setup_ones, 1)

            def rstd_1(b):
                if on(b):
                    pool.wait_ge(var_ready, b + 1)
                    after(pool, x_normed, NU * b)
                    nc.gpsimd.tensor_tensor(rstd[:, 0, :], ve[:, 0, :], mhalf[:, 0:1].broadcast_to([P, NU]),
                                            ALU.pow).then_inc(rstd_ready, 1)

            def rstd_2(b, u):
                if on(b):
                    pool.wait_ge(var2_ready, NU * b + u + 1)
                    after(pool, xn_ready, NU * (b - 1) + u + 1)
                    nc.gpsimd.tensor_tensor(rstd[:, 1, u:u + 1], ve[:, 1, u:u + 1], mhalf[:, 0:1],
                                            ALU.pow).then_inc(rstd2_ready, 1)

            def k_low(b, c, *before):
                if on(b):
                    for s, count in before:
                        after(pool, s, count)
                    pool.wait_ge(k_pos, CH * b + c + 1)
                    pool.wait_ge(k_hi_ready, CH * b + c + 1)
                    rows = slice(2 * HD, 3 * HD)
                    nc.gpsimd.tensor_tensor(k_st[rows, c, :, :], k_raw[rows, :, :], k_st[rows, c, :, :].bitcast(F32),
                                            ALU.subtract).then_inc(k_lo_ready, 1)
                    pool.wait_ge(k_lo_ready, CH * b + c + 1)

            def o_low(b, u):
                if on(b):
                    pool.wait_ge(o_hi_ready, NU * b + u + 1)
                    after(pool, z_ready, NU * (b - 1) + u + 1)
                    nc.gpsimd.tensor_tensor(by_tile(o_lo, u), o_mv[:, :, :].rearrange("p g (k a) -> p k g a", k=KC),
                                            by_tile(o_hi, u).bitcast(F32), ALU.subtract).then_inc(o_lo_ready, 1)

            def x_diff(b, u):
                if on(b):
                    pool.wait_ge(xt_ready, NU * b + u + 1)
                    after(pool, xr_hi_ready, b)
                    after(pool, xr_lo_ready, b)
                    nc.gpsimd.tensor_tensor(xd[:, :, P * u:P * u + P], xt[:, :, 1 + P * u:1 + P * u + P],
                                            xt[:, :, P * u:P * u + P], ALU.subtract).then_inc(xd_ready, 1)

            def xk_low(b, half):
                if on(b):
                    pool.wait_ge(xk_ready, 2 * b + half + 1)
                    pool.wait_ge(xk_hi_ready, 2 * b + half + 1)
                    after(pool, kt_ready, 2 * b)
                    part = slice(2 * half, 2 * half + 2)
                    nc.gpsimd.tensor_tensor(xk_lo[:, part, :], xm[:, part, :], xk_hi[:, part, :].bitcast(F32),
                                            ALU.subtract).then_inc(xk_lo_ready, 1)

            def xr_low(b):
                if on(b):
                    pool.wait_ge(xr_ready, b + 1)
                    pool.wait_ge(xr_hi_ready, b + 1)
                    after(pool, r_ready, NU * b)
                    nc.gpsimd.tensor_tensor(xr_lo[:, :, :], xd[:, :, :], xr_hi[:, :, :].bitcast(F32),
                                            ALU.subtract).then_inc(xr_lo_ready, 1)

            def ka_square(b, half):
                if on(b):
                    pool.wait_ge(kt_relued, 2 * b + half + 1)
                    part = xm[:, 2 * half:2 * half + 2, :]
                    nc.gpsimd.tensor_tensor(part, part, part, ALU.mult).then_inc(ka_ready, 1)

            def ka_low(b, half):
                if on(b):
                    pool.wait_ge(ka_ready, 2 * b + half + 1)
                    pool.wait_ge(ka_hi_ready, 2 * b + half + 1)
                    after(pool, vv_ready, NU * b)
                    nc.gpsimd.tensor_tensor(ka_lo[:, 2 * half:2 * half + 2, :], xm[:, 2 * half:2 * half + 2, :],
                                            ka_hi[:, 2 * half:2 * half + 2, :].bitcast(F32),
                                            ALU.subtract).then_inc(ka_lo_ready, 1)

            def iteration(i, par):
                for s in range(STEPS):
                    if s == 1:
                        xr_low(i - 2)
                    if s == 2:
                        k_low(i, 3, (xr_lo_ready, i - 1), (o_lo_ready, NU * (i - 1) + 1))
                    if s == 3:
                        ka_square(i - 2, 0)
                        rstd_1(i + 1)
                    if s == 4:
                        o_low(i - 1, 1)
                    if s == 5:
                        ka_low(i - 2, 0)
                        ka_square(i - 2, 1)
                    if s == 6:
                        k_low(i + 1, 0, (ka_ready, 2 * (i - 2) + 2), (o_lo_ready, NU * i), (rstd_ready, i + 2))
                        rstd_2(i - 1, 0)
                    if s == 7:
                        ka_low(i - 2, 1)
                    if s == 8:
                        rstd_2(i - 1, 1)
                    if s == 10:
                        x_diff(i - 1, 0)
                        x_diff(i - 1, 1)
                    if s == 11:
                        k_low(i + 1, 1, (xd_ready, NU * i), (ka_lo_ready, 2 * (i - 2) + 2))
                    if s == 13:
                        xk_low(i - 1, 0)
                        xk_low(i - 1, 1)
                    if s == 15:
                        k_low(i + 1, 2, (xk_lo_ready, 2 * i))
                        o_low(i, 0)

            pipeline(pool, iteration)

        @block.scalar
        def _(act):
            act.wait_ge(setup_loaded, 80)
            nc.scalar.activation(tg[:, :], gates[:, :], ACT.Tanh).then_inc(setup_act, 1)
            act.wait_ge(setup_pool, 2)
            act.wait_ge(setup_ones, 1)
            nc.scalar.activation(ident_r[:, :], ident_raw, ACT.Copy).then_inc(setup_act, 1)
            nc.scalar.activation(b_rows[0:1, :], b_raw, ACT.Copy).then_inc(setup_act, 1)
            for n in range(4):
                act.wait_ge(w_loaded[n % 2], 16 * (n // 2 + 1))
                nc.scalar.activation(w_hi[n][:, :, :].rearrange("p c n -> p (c n)"), w_raw[n % 2],
                                     ACT.Copy).then_inc(setup_act, 1)
            act.wait_ge(setup_dve, 6)
            act.wait_ge(b_low_moved, 16)

            def load_x1(b, par):
                if on(b):
                    after(act, stored, 16 * (b - 1))
                    act.dma_start(x1[:, par, :, :], x[b].rearrange("(u p) d -> p u d", p=P)).then_inc(x1_loaded, 16)

            def q_high(b, u):
                if on(b):
                    act.wait_ge(x_normed, NU * b + u + 1)
                    after(act, q_turned, 2 * CH * b)
                    xu = x_ln[:, u, :].rearrange("p (h f) -> p h f", h=HEADS)
                    nc.scalar.activation(q_nat[:, u, :, 0, :], xu, ACT.Relu)
                    nc.scalar.activation(q_nat[:, u, :, 2, :], xu, ACT.Relu).then_inc(q_hi_ready, 1)

            def q_stack(b, c, u):
                if on(b):
                    act.wait_ge(q_turned, 2 * CH * b + 2 * c + u + 1)
                    after(act, st_ready, HEADS * (b - 1) + GR * c + GR)
                    nc.scalar.activation(q_st[0:QK, c, :, P * u:P * u + P],
                                         tp_bank[0:QK, :].rearrange("p (g t) -> p g t", g=GR),
                                         ACT.Copy).then_inc(q_stacked, 1)

            def k_high(b, c):
                if on(b):
                    act.wait_ge(k_loaded, 48 * (CH * b + c + 1))
                    after(act, st_ready, HEADS * (b - 1) + GR * c + GR)
                    nc.scalar.activation(k_st[0:QK, c, :, :], k_raw[0:QK, :, :], ACT.Relu).then_inc(k_hi_ready, 1)
                    rows = slice(2 * HD, 3 * HD)
                    act.wait_ge(k_hi_ready, CH * b + c + 1)
                    nc.scalar.activation(k_raw[rows, :, :], k_raw[rows, :, :], ACT.Relu).then_inc(k_pos, 1)

            def exponent(b, n):
                if on(b):
                    act.wait_ge(st_ready, HEADS * b + n + 1)
                    if n % GR == 0:
                        after(act, pv_ready, CH * b + n // GR - 1)
                    nc.scalar.activation(probs[:, n // GR % 2, n % GR, :, :].rearrange("p v t -> p (v t)"),
                                         st_bank[n % 2][:, :], ACT.Exp, scale=SCALE).then_inc(exp_ready, 1)

            def o_high(b, u):
                if on(b):
                    act.wait_ge(o_moved, 16 * GR * (NU * b + u + 1))
                    after(act, z_ready, NU * (b - 1) + u + 1)
                    nc.scalar.activation(by_tile(o_hi, u), o_mv[:, :, :].rearrange("p g (k a) -> p k g a", k=KC),
                                         ACT.Copy).then_inc(o_hi_ready, 1)

            def z_relu(b, u):
                if on(b):
                    act.wait_ge(z_ready, NU * b + u + 1)
                    after(act, xn_turned, NU * (b - 1) + u + 1)
                    nc.scalar.activation(xn[:, u, :], dense_bank[u][:, :], ACT.Relu).then_inc(z_relued, 1)

            def xt_copy(b, u):
                if on(b):
                    act.wait_ge(xn_turned, NU * b + u + 1)
                    after(act, xr_ready, b)
                    nc.scalar.activation(xt[:, :, 1 + P * u:1 + P * u + P],
                                         tp_bank[:, :].rearrange("p (c t) -> p c t", c=KC),
                                         ACT.Copy).then_inc(xt_ready, 1)

            def xk_high(b, half):
                if on(b):
                    act.wait_ge(xk_ready, 2 * b + half + 1)
                    after(act, kt_ready, 2 * b)
                    part = slice(2 * half, 2 * half + 2)
                    nc.scalar.activation(xk_hi[:, part, :], xm[:, part, :], ACT.Copy).then_inc(xk_hi_ready, 1)

            def xr_high(b):
                if on(b):
                    act.wait_ge(xr_ready, b + 1)
                    after(act, r_ready, NU * b)
                    nc.scalar.activation(xr_hi[:, :, :], xd[:, :, :], ACT.Copy).then_inc(xr_hi_ready, 1)

            def kt_relu(b, half):
                if on(b):
                    act.wait_ge(kt_ready, 2 * b + half + 1)
                    act.wait_ge(xk_lo_ready, 2 * b + 2)
                    nc.scalar.activation(xm[:, 2 * half:2 * half + 2, :].rearrange("p c t -> p (c t)"),
                                         dense_bank[half][:, :], ACT.Relu).then_inc(kt_relued, 1)

            def ka_high(b, half):
                if on(b):
                    act.wait_ge(ka_ready, 2 * b + half + 1)
                    after(act, vv_ready, NU * b)
                    nc.scalar.activation(ka_hi[:, 2 * half:2 * half + 2, :], xm[:, 2 * half:2 * half + 2, :],
                                         ACT.Copy).then_inc(ka_hi_ready, 1)

            def r_tanh(b, u):
                if on(b):
                    act.wait_ge(r_ready, NU * b + u + 1)
                    after(act, out_ready, NU * (b - 1) + u + 1)
                    nc.scalar.activation(th[:, u, :], dense_bank[u][:, :], ACT.Tanh,
                                         scale=0.5).then_inc(th_ready, 1)

            def iteration(i, par):
                for s in range(STEPS):
                    if s == 0:
                        q_stack(i, 2, 1)
                    if s == 3:
                        q_stack(i, 3, 0)
                    if s == 4:
                        q_stack(i, 3, 1)
                    if s == 7:
                        q_stack(i + 1, 0, 0)
                    if s == 8:
                        q_stack(i + 1, 0, 1)
                    if s == 10:
                        xt_copy(i - 1, 0)
                    if s == 11:
                        xt_copy(i - 1, 1)
                    if s == 12:
                        q_stack(i + 1, 1, 0)
                    if s == 13:
                        q_stack(i + 1, 1, 1)
                    if s == 15:
                        q_stack(i + 1, 2, 0)
                    exponent(i, s)
                    if s == 0:
                        xr_high(i - 2)
                    if s == 1:
                        k_high(i, 3)
                    if s == 2:
                        kt_relu(i - 2, 0)
                    if s == 3:
                        load_x1(i - 1, 1 - par)
                    if s == 4:
                        kt_relu(i - 2, 1)
                        o_high(i - 1, 1)
                        ka_high(i - 2, 0)
                    if s == 5:
                        q_high(i + 1, 0)
                        q_high(i + 1, 1)
                        k_high(i + 1, 0)
                    if s == 6:
                        z_relu(i - 1, 0)
                        ka_high(i - 2, 1)
                    if s == 8:
                        z_relu(i - 1, 1)
                    if s == 9:
                        k_high(i + 1, 1)
                    if s == 10:
                        r_tanh(i - 2, 0)
                    if s == 12:
                        r_tanh(i - 2, 1)
                    if s == 13:
                        xk_high(i - 1, 0)
                        xk_high(i - 1, 1)
                    if s == 14:
                        k_high(i + 1, 2)
                        o_high(i, 0)

            pipeline(act, iteration)

        @block.vector
        def _(dve):
            nc.vector.memset(b_rows[:, :].bitcast(F32), 0.0)
            nc.vector.memset(ones_r[:, :].bitcast(F32), 1.0)
            nc.vector.memset(mhalf[:, :], -0.5)
            nc.vector.memset(xt[:, :, 0:1], 0.0)
            nc.vector.memset(k_st[QK:P, :, :, :].bitcast(F32), 1.0).then_inc(setup_ones, 1)
            dve.wait_ge(setup_act, 3)
            nc.vector.tensor_tensor(b_low, b_raw, b_rows[0:1, :].bitcast(F32), ALU.subtract).then_inc(setup_dve, 1)
            nc.vector.tensor_scalar(tgh[:, :], tg[:, 1:2], 0.5, None, ALU.mult).then_inc(setup_dve, 1)
            for n in range(4):
                dve.wait_ge(setup_act, 4 + n)
                nc.vector.tensor_tensor(w_lo[n][:, :, :].rearrange("p c n -> p (c n)"), w_raw[n % 2],
                                        w_hi[n][:, :, :].rearrange("p c n -> p (c n)").bitcast(F32),
                                        ALU.subtract).then_inc(setup_dve, 1)
            dve.wait_ge(setup_dve, 6)

            def stats_1(b):
                if on(b):
                    dve.wait_ge(x_loaded, 16 * GR * (b + 1))
                    for u in range(NU):
                        last = nc.vector.bn_stats(st6[:, 0, u, :], x_ln[:, u, :])
                    last.then_inc(stat1, 1)
                    dve.wait_ge(stat1, b + 1)
                    nc.vector.memset(carrier[:, :], 0.0)
                    for u in range(NU):
                        last = nc.vector.bn_aggr(mv[:, 0, u, :], st6[:, 0, u, :])
                    last.then_inc(mv1, 1)
                    dve.wait_ge(mv1, b + 1)
                    after(dve, rstd_ready, b)
                    nc.vector.tensor_scalar(ve[:, 0, :], mv[:, 0, :, 1], LN_EPS, None, ALU.add).then_inc(var_ready, 1)

            def norm_1(b):
                if on(b):
                    dve.wait_ge(rstd_ready, b + 1)
                    for u in range(NU):
                        nc.vector.tensor_scalar(x_ln[:, u, :], x_ln[:, u, :], mv[:, 0, u, 0:1], rstd[:, 0, u:u + 1],
                                                ALU.subtract, ALU.mult).then_inc(x_normed, 1)

            def q_low(b, u):
                if on(b):
                    dve.wait_ge(q_hi_ready, NU * b + u + 1)
                    nc.vector.scalar_tensor_tensor(out=q_nat[:, u, :, 1, :],
                                                   in0=x_ln[:, u, :].rearrange("p (h f) -> p h f", h=HEADS), scalar=0.0,
                                                   in1=q_nat[:, u, :, 0, :].bitcast(F32), op0=ALU.max,
                                                   op1=ALU.subtract).then_inc(q_lo_ready, 1)

            def relu_v(b, par):
                if on(b):
                    dve.wait_ge(v_loaded[par], 8 * (b - par) + 16)
                    part = v_pos[:, par, :, :]
                    nc.vector.tensor_scalar(part, part, 0.0, None, ALU.max).then_inc(v_ready, 1)

            def head_max(b, n):
                if on(b):
                    dve.wait_ge(s_ready, HEADS * b + n + 1)
                    if n % GR == 0:
                        after(dve, m_split, CH * b + n // GR)
                    nc.vector.tensor_reduce(nmax[:, :, n % GR:n % GR + 1],
                                            s_bank[n % 2][:, :].rearrange("p (u y) -> p u y", u=NU),
                                            AX_X, ALU.max, negate=True).then_inc(s_maxed, 1)

            def split_m(b, c):
                if on(b):
                    dve.wait_ge(s_maxed, HEADS * b + GR * c + GR)
                    after(dve, m_turned, CH * b + c)
                    nc.vector.tensor_copy(m_nat[:, :, 0, :], nmax[:, :, :]).then_inc(m_hi_ready, 1)
                    dve.wait_ge(m_hi_ready, CH * b + c + 1)
                    nc.vector.tensor_tensor(m_nat[:, :, 1, :], nmax[:, :, :], m_nat[:, :, 0, :].bitcast(F32),
                                            ALU.subtract).then_inc(m_split, 1)

            def copy_m(b, c):
                if on(b):
                    dve.wait_ge(m_turned, CH * b + c + 1)
                    after(dve, m_moved[(c + 1) % 2], 32 * (2 * b + (c + 1) // 2))
                    nc.vector.tensor_copy(m_t[0:2 * GR, :], tp_bank[0:2 * GR, 0:T]).then_inc(m_copied, 1)

            def norm_o(b, c):
                if on(b):
                    dve.wait_ge(pv_ready, CH * b + c + 1)
                    after(dve, o_written, 16 * (CH * b + c))
                    if c % 2 == 1:
                        after(dve, o_lo_ready, NU * b + c // 2)
                    nc.vector.reciprocal(o_val[:, :], pv_bank[:, T:2 * T]).then_inc(rden_ready, 1)
                    dve.wait_ge(rden_ready, CH * b + c + 1)
                    nc.vector.tensor_tensor(o_val[:, :], pv_bank[:, 0:T], o_val[:, :],
                                            ALU.mult).then_inc(o_ready, 1)

            def add_x(b, u, par):
                if on(b):
                    dve.wait_ge(z_relued, NU * b + u + 1)
                    dve.wait_ge(x1_loaded, 16 * (b + 1))
                    nc.vector.scalar_tensor_tensor(out=x1[:, par, u, :], in0=xn[:, u, :], scalar=tg[:, 0:1],
                                                   in1=x1[:, par, u, :], op0=ALU.mult, op1=ALU.add).then_inc(x1_ready, 1)
                    dve.wait_ge(x1_ready, NU * b + u + 1)
                    nc.vector.bn_stats(st6[:, 1, u, :], x1[:, par, u, :]).then_inc(stat2, 1)
                    dve.wait_ge(stat2, NU * b + u + 1)
                    nc.vector.memset(carrier[:, :], 0.0)
                    nc.vector.bn_aggr(mv[:, 1, u, :], st6[:, 1, u, :]).then_inc(mv2, 1)
                    dve.wait_ge(mv2, NU * b + u + 1)
                    after(dve, rstd2_ready, NU * (b - 1) + u + 1)
                    nc.vector.tensor_scalar(ve[:, 1, u:u + 1], mv[:, 1, u, 1:2], LN_EPS, None,
                                            ALU.add).then_inc(var2_ready, 1)

            def norm_2(b, u, par):
                if on(b):
                    dve.wait_ge(rstd2_ready, NU * b + u + 1)
                    nc.vector.tensor_scalar(xn[:, u, :], x1[:, par, u, :], mv[:, 1, u, 0:1], rstd[:, 1, u:u + 1],
                                            ALU.subtract, ALU.mult).then_inc(xn_ready, 1)

            def mix_k(b):
                if on(b):
                    dve.wait_ge(xd_ready, NU * (b + 1))
                    after(dve, ka_lo_ready, 2 * b)
                    for half in range(2):
                        for c in (2 * half, 2 * half + 1):
                            last = nc.vector.scalar_tensor_tensor(out=xm[:, c, :], in0=xd[:, c, :],
                                                                  scalar=mu_sb[:, 1, c:c + 1], in1=xt[:, c, 0:T],
                                                                  op0=ALU.mult, op1=ALU.add)
                        last.then_inc(xk_ready, 1)

            def mix_r(b):
                if on(b):
                    dve.wait_ge(xk_ready, 2 * (b + 1))
                    for c in range(KC):
                        last = nc.vector.scalar_tensor_tensor(out=xd[:, c, :], in0=xd[:, c, :], scalar=mu_sb[:, 0, c:c + 1],
                                                              in1=xt[:, c, 0:T], op0=ALU.mult, op1=ALU.add)
                    last.then_inc(xr_ready, 1)

            def finish(b, u, par):
                if on(b):
                    dve.wait_ge(vv_ready, NU * b + u + 1)
                    dve.wait_ge(th_ready, NU * b + u + 1)
                    nc.vector.scalar_tensor_tensor(out=th[:, u, :], in0=th[:, u, :], scalar=1.0,
                                                   in1=dense_bank[u][:, :], op0=ALU.add, op1=ALU.mult).then_inc(y_ready, 1)
                    dve.wait_ge(y_ready, NU * b + u + 1)
                    nc.vector.scalar_tensor_tensor(out=x1[:, par, u, :], in0=th[:, u, :], scalar=tgh[:, 0:1],
                                                   in1=x1[:, par, u, :], op0=ALU.mult, op1=ALU.add).then_inc(out_ready, 1)

            def iteration(i, par):
                for s in range(STEPS):
                    c = s // 4
                    if s in (1, 5, 9):
                        copy_m(i, c + 1)
                    if s == 9:
                        norm_2(i - 1, 1, 1 - par)
                    if s % 4 == 1:
                        norm_o(i if c >= 1 else i - 1, (c - 1) % CH)
                    if s == 14:
                        copy_m(i + 1, 0)
                        finish(i - 2, 0, par)
                    if s == 0:
                        finish(i - 3, 1, 1 - par)
                    if s == 2:
                        stats_1(i + 1)
                    if s == 4:
                        norm_1(i + 1)
                    if s == 6:
                        q_low(i + 1, 0)
                    if s == 7:
                        q_low(i + 1, 1)
                        add_x(i - 1, 0, 1 - par)
                    if s == 11:
                        relu_v(i + 1, 1 - par)
                    if s == 12:
                        mix_k(i - 1)
                    if s == 15:
                        mix_r(i - 1)
                    n = s + AHEAD
                    head_max(i if n < HEADS else i + 1, n % HEADS)
                    if s % 4 == 0:
                        split_m(i if c + 1 < CH else i + 1, (c + 1) % CH)
                    if s == 7:
                        norm_2(i - 1, 0, 1 - par)
                    if s == 8:
                        add_x(i - 1, 1, 1 - par)

            pipeline(dve, iteration)

        @block.tensor
        def _(pe):
            pe.wait_ge(setup_act, 7)
            pe.wait_ge(setup_dve, 6)
            pe.wait_ge(setup_pool, 2)
            pe.wait_ge(setup_ones, 1)
            pe.wait_ge(b_low_moved, 16)

            def freed(*copies):
                for s, b, per, k in copies:
                    if on(b):
                        after(pe, s, b * per + k)
                        break

            def turn_q(b, c, u, *users):
                if on(b):
                    pe.wait_ge(q_hi_ready, NU * b + u + 1)
                    pe.wait_ge(q_lo_ready, NU * b + u + 1)
                    freed(*users)
                    for g in range(GR):
                        mm = nc.tensor.transpose(tp_bank[0:QK, P * g:P * g + P].bitcast(F32R),
                                                 q_nat[:, u, GR * c + g, :, :], ident_r[:, :])
                    mm.then_inc(q_turned, 1)

            def turn_m(b, c, *users):
                if on(b):
                    pe.wait_ge(m_split, CH * b + c + 1)
                    freed(*users)
                    for u in range(NU):
                        mm = nc.tensor.transpose(tp_bank[0:2 * GR, P * u:P * u + P].bitcast(F32R),
                                                 m_nat[:, u, :, :], ident_r[:, :])
                    mm.then_inc(m_turned, 1)

            def turn_xn(b, u, *users):
                if on(b):
                    pe.wait_ge(xn_ready, NU * b + u + 1)
                    freed(*users)
                    for c in range(KC):
                        mm = nc.tensor.transpose(tp_bank[:, P * c:P * c + P], xn[:, u, P * c:P * c + P],
                                                 ident_r[:, :].bitcast(F32))
                    mm.then_inc(xn_turned, 1)

            def scores(b, n):
                if on(b):
                    c, g = n // GR, n % GR
                    if g == 0:
                        pe.wait_ge(q_stacked, 2 * CH * b + 2 * c + 2)
                        pe.wait_ge(k_hi_ready, CH * b + c + 1)
                        pe.wait_ge(k_lo_ready, CH * b + c + 1)
                    after(pe, s_maxed, HEADS * b + n - 1)
                    for u in range(NU):
                        mm = nc.tensor.matmul(s_bank[n % 2][:, T * u:T * u + T], q_st[0:QK, c, g, P * u:P * u + P],
                                              k_st[0:QK, c, g, :], start=True, stop=True)
                    mm.then_inc(s_ready, 1)

            def shifted_scores(b, n):
                if on(b):
                    c, g = n // GR, n % GR
                    if g == 0:
                        pe.wait_ge(m_moved[c % 2], 32 * (2 * b + c // 2 + 1))
                    after(pe, exp_ready, HEADS * b + n - 1)
                    for v in range(NU):
                        mm = nc.tensor.matmul(st_bank[n % 2][:, T * v:T * v + T], k_st[0:ST, c, g, P * v:P * v + P],
                                              q_st[0:ST, c, g, :], start=True, stop=True)
                    mm.then_inc(st_ready, 1)

            def values(b, c, par):
                if on(b):
                    pe.wait_ge(exp_ready, HEADS * b + GR * c + GR)
                    pe.wait_ge(v_ready, b + 1)
                    after(pe, o_ready, CH * b + c)
                    for v in range(NU):
                        for g in range(GR):
                            h = GR * c + g
                            nc.tensor.matmul(pv_bank[HD * g:HD * g + HD, 0:T], v_pos[:, par, v, HD * h:HD * h + HD],
                                             probs[:, c % 2, g, v, :], start=(v == 0), stop=(v == NU - 1))
                    for v in range(NU):
                        for g in range(GR):
                            mm = nc.tensor.matmul(pv_bank[HD * g:HD * g + HD, T:2 * T], ones_r[:, 0:HD].bitcast(F32),
                                                  probs[:, c % 2, g, v, :], start=(v == 0), stop=(v == NU - 1))
                    mm.then_inc(pv_ready, 1)

            def product(dst, lhs, rhs, first, last):
                for n, (a, c) in enumerate(((0, 0), (1, 0), (0, 1))):
                    mm = nc.tensor.matmul(dst, lhs[a], rhs[c], start=first and n == 0, stop=last and n == 2)
                return mm

            def project(b, u, part, *users):
                if on(b):
                    if part == 0:
                        freed(*users)
                        nc.tensor.matmul(dense_bank[u][:, :], ones_r[:, :], b_rows[:, :], start=True, stop=False)
                        pe.wait_ge(o_hi_ready, NU * b + u + 1)
                        pe.wait_ge(o_lo_ready, NU * b + u + 1)
                    rows = slice(P * u, P * u + P)
                    mm = product(dense_bank[u][:, :], (o_hi[:, part, rows], o_lo[:, part, rows]),
                                 (w_hi[W_X][:, part, :], w_lo[W_X][:, part, :]), False, part == KC - 1)
                    if part == KC - 1:
                        mm.then_inc(z_ready, 1)

            def receptance(b, u, part, *users):
                if on(b):
                    if part == 0:
                        freed(*users)
                        pe.wait_ge(xr_hi_ready, b + 1)
                        pe.wait_ge(xr_lo_ready, b + 1)
                    rows = slice(P * u, P * u + P)
                    mm = product(dense_bank[u][:, :], (xr_hi[:, part, rows], xr_lo[:, part, rows]),
                                 (w_hi[W_R][:, part, :], w_lo[W_R][:, part, :]), part == 0, part == KC - 1)
                    if part == KC - 1:
                        mm.then_inc(r_ready, 1)

            def key(b, half, part, *users):
                if on(b):
                    if part == 0:
                        freed(*users)
                    if half == 0 and part < 2:
                        pe.wait_ge(xk_hi_ready, 2 * b + part + 1)
                        pe.wait_ge(xk_lo_ready, 2 * b + part + 1)
                    m = part // 2
                    n = 2 * half + m
                    cols = slice(P * n, P * n + P)
                    for kc in (2 * (part % 2), 2 * (part % 2) + 1):
                        mm = product(dense_bank[half][:, T * m:T * m + T],
                                     (w_hi[W_K][:, kc, cols], w_lo[W_K][:, kc, cols]),
                                     (xk_hi[:, kc, :], xk_lo[:, kc, :]), kc == 0, kc == KC - 1)
                    if part == 3:
                        mm.then_inc(kt_ready, 1)

            def value(b, u, part, *users):
                if on(b):
                    if part == 0:
                        freed(*users)
                    if part % 2 == 0:
                        pe.wait_ge(ka_hi_ready, 2 * b + part // 2 + 1)
                        pe.wait_ge(ka_lo_ready, 2 * b + part // 2 + 1)
                    rows = slice(P * u, P * u + P)
                    mm = product(dense_bank[u][:, :], (ka_hi[:, part, rows], ka_lo[:, part, rows]),
                                 (w_hi[W_V][:, part, :], w_lo[W_V][:, part, :]), part == 0, part == KC - 1)
                    if part == KC - 1:
                        mm.then_inc(vv_ready, 1)

            def iteration(i, par):
                def dense(q, part):
                    b1, b2, u = i - 1, i - 2, q % 2
                    if q < 2:
                        key(b2, u, part, (y_ready, i - 3, NU, u + 1), (z_relued, b2, NU, u + 1))
                    elif q < 4:
                        project(b1, u, part, (kt_relued, b2, 2, u + 1))
                    elif q < 6:
                        receptance(b2, u, part, (z_relued, b1, NU, u + 1), (kt_relued, b2, 2, u + 1))
                    else:
                        value(b2, u, part, (th_ready, b2, NU, u + 1))

                turns = [(0, "q", i, 2, 1), (1, "m", i, 1, 0), (3, "q", i, 3, 0), (4, "q", i, 3, 1), (5, "m", i, 2, 0),
                         (7, "q", i + 1, 0, 0), (8, "q", i + 1, 0, 1), (9, "m", i, 3, 0), (9.5, "x", i - 1, 0, 0),
                         (10.5, "x", i - 1, 0, 1), (11.5, "q", i + 1, 1, 0), (12.5, "q", i + 1, 1, 1),
                         (13.5, "m", i + 1, 0, 0), (15, "q", i + 1, 2, 0)]

                def copy_of(kind, b, c, u):
                    if kind == "q":
                        return q_stacked, b, 2 * CH, 2 * c + u + 1
                    if kind == "m":
                        return m_copied, b, CH, c + 1
                    return xt_ready, b, NU, u + 1

                def turn(n):
                    _, kind, b, c, u = turns[n]
                    users = [copy_of(*t[1:]) for t in reversed(turns[:n])]
                    users += [copy_of(t[1], t[2] - 1, *t[3:]) for t in reversed(turns)]
                    if kind == "q":
                        turn_q(b, c, u, *users)
                    elif kind == "m":
                        turn_m(b, c, *users)
                    else:
                        turn_xn(b, u, *users)

                for s in range(STEPS):
                    for n, t in enumerate(turns):
                        if t[0] == s:
                            turn(n)
                    shifted_scores(i, s)
                    dense(s // 2, 2 * (s % 2))
                    for n, t in enumerate(turns):
                        if t[0] == s + 0.5:
                            turn(n)
                    n = s + AHEAD
                    scores(i if n < HEADS else i + 1, n % HEADS)
                    dense(s // 2, 2 * (s % 2) + 1)
                    if s % 4 == 0:
                        values(i if s >= 4 else i - 1, (s // 4 - 1) % CH, par if s >= 4 else 1 - par)

            pipeline(pe, iteration)


def kernel(**inputs):
    import numpy as np
    import concourse.bacc as bacc
    from concourse.bass_utils import run_bass_kernel_spmd

    x = np.asarray(inputs["x"])
    ctx_in = np.asarray(inputs["ctx_1024"])
    nb, t, d = ctx_in.shape
    ctx_t = ctx_in.reshape(nb, t, HEADS, d // HEADS).transpose(0, 3, 2, 1)
    arrays = {
        "x": x,
        "ctx": ctx_in,
        "ctx_t": ctx_t,
        "g_xattn": np.asarray(inputs["g_xattn"]),
        "g_ffn": np.asarray(inputs["g_ffn"]),
        "w_x": np.asarray(inputs["L0_xattn_ffn_w"]).T,
        "w_r": np.asarray(inputs["L0_ffn_W_r"]).T,
        "w_k": np.asarray(inputs["L0_ffn_W_k"]).T,
        "w_v": np.asarray(inputs["L0_ffn_W_v"]).T,
        "bias": np.asarray(inputs["L0_xattn_ffn_b"]),
        "mu_r": np.asarray(inputs["L0_ffn_mu_r"]).reshape(-1, P).T,
        "mu_k": np.asarray(inputs["L0_ffn_mu_k"]).reshape(-1, P).T,
    }
    arrays = {name: np.ascontiguousarray(a) for name, a in arrays.items()}
    nc = bacc.Bacc("TRN2", target_bir_lowering=False, num_devices=1)
    h = {name: nc.dram_tensor(name + "_dram", a.shape, mybir.dt.from_np(a.dtype), kind="ExternalInput").ap()
         for name, a in arrays.items()}
    out = nc.dram_tensor("out_dram", x.shape, mybir.dt.from_np(x.dtype), kind="ExternalOutput").ap()
    flamingo_block(nc, h["x"], h["ctx"], h["ctx_t"], h["g_xattn"], h["g_ffn"],
                   [h["w_x"], h["w_r"], h["w_k"], h["w_v"]], h["bias"], [h["mu_r"], h["mu_k"]], out)
    r = run_bass_kernel_spmd(nc, [{name + "_dram": a for name, a in arrays.items()}], core_ids=[0])
    return r.results[0]["out_dram"]
```

```python
from contextlib import ExitStack

import concourse.bass as bass
from concourse import mybir

F32 = mybir.dt.float32
F32R = mybir.dt.float32r
ALU = mybir.AluOpType
ACT = mybir.ActivationFunctionType
AX_X = mybir.AxisListType.X

P = 128
HEADS = 16
LN_EPS = 1e-5


def flamingo_block(nc, x, ctx_in, ctx_t, g_xattn, g_ffn, w_t, bias, mu, out):
    NB, T, D = x.shape
    HD = D // HEADS
    NU = T // P
    KC = D // P
    GR = P // HD
    CH = HEADS // GR
    SCALE = float(HD) ** -0.5
    assert NU == 2 and KC == 4 and GR == 4 and CH == 4 and HD == 32
    QK = 3 * HD
    ST = QK + 2

    es = ExitStack()
    with es:
        def sb(name, shape, dt=F32):
            return es.enter_context(nc.sbuf_tensor(name, shape, dt))

        def sem(name):
            return es.enter_context(nc.semaphore(name))

        o_dram = nc.dram_tensor("o_dram", [CH, GR, HD, GR, T // GR], F32, kind="Internal").ap()

        w_hi = [sb(f"w_hi{n}", [P, KC, D], F32R) for n in range(4)]
        w_lo = [sb(f"w_lo{n}", [P, KC, D], F32R) for n in range(4)]
        W_X, W_R, W_K, W_V = range(4)
        x_ln = sb("x_ln", [P, NU, D])
        q_nat = sb("q_nat", [P, NU, HEADS, 3, HD], F32R)
        v_pos = sb("v_pos", [P, NU, D])
        k_raw = sb("k_raw", [P, GR, T])
        k_st = sb("k_st", [P, CH, GR, T], F32R)
        q_st = sb("q_st", [P, CH, GR, T], F32R)
        probs = sb("probs", [P, 2, GR, NU, T])
        p_sum = sb("p_sum", [P, GR, T])
        o_val = sb("o_val", [P, T])
        o_mv = sb("o_mv", [P, 2 * GR, T // GR])
        o_hi = sb("o_hi", [P, KC, T], F32R)
        o_lo = sb("o_lo", [P, KC, T], F32R)
        x1 = sb("x1", [P, 2, NU, D])
        xn = sb("xn", [P, NU, D])
        xt = sb("xt", [P, KC, T + 1])
        xd = sb("xd", [P, KC, T])
        xm = sb("xm", [P, KC, T])
        xr_hi = sb("xr_hi", [P, KC, T], F32R)
        xr_lo = sb("xr_lo", [P, KC, T], F32R)
        xk_hi = sb("xk_hi", [P, KC, T], F32R)
        xk_lo = sb("xk_lo", [P, KC, T], F32R)
        ka_hi = sb("ka_hi", [P, KC, T], F32R)
        ka_lo = sb("ka_lo", [P, KC, T], F32R)
        th = sb("th", [P, NU, D])
        b_rows = sb("b_rows", [P, D], F32R)
        ones_r = sb("ones_r", [P, P], F32R)
        ident_r = sb("ident_r", [P, P], F32R)
        m_t = sb("m_t", [P, T], F32R)
        nmax = sb("nmax", [P, NU, GR])
        m_nat = sb("m_nat", [P, NU, 2, GR], F32R)
        st6 = sb("st6", [P, 2, NU, 6])
        mv = sb("mv", [P, 2, NU, 2])
        ve = sb("ve", [P, 2, NU])
        rstd = sb("rstd", [P, 2, NU])
        carrier = sb("carrier", [P, 1])
        mhalf = sb("mhalf", [P, 1])
        mu_sb = sb("mu_sb", [P, 2, KC])
        gates = sb("gates", [P, 2])
        tg = sb("tg", [P, 2])
        tgh = sb("tgh", [P, 1])
        w_raw = [probs[:, 1, 0:2, :, :].rearrange("p g v t -> p (g v) t"),
                 probs[:, 1, 2:4, :, :].rearrange("p g v t -> p (g v) t"),
                 x1[:, 0, :, :], x1[:, 1, :, :], xm[:, :, :], xd[:, :, :], th[:, :, :], xn[:, :, :]]
        w_raw = [a.rearrange("p a b -> p (a b)") for a in w_raw]
        ident_raw = xn[:, 0, 0:P]
        b_raw = th[0:1, 0, :]
        b_low = th[0:1, 1, :].bitcast(F32R)

        bank = [es.enter_context(nc.psum_tensor(f"bank{n}", [P, 512], F32)) for n in range(8)]
        s_bank, st_bank, pv_bank, dense_bank, tp_bank = bank[0:2], bank[2:4], bank[4], bank[5:7], bank[7]

        x_loaded = sem("x_loaded")
        v_loaded = sem("v_loaded")
        k_loaded = sem("k_loaded")
        x1_loaded = sem("x1_loaded")
        m_moved = [sem("m_moved0"), sem("m_moved1")]
        stored = sem("stored")
        setup_loaded = sem("setup_loaded")
        w_loaded = [sem(f"w_loaded{n}") for n in range(8)]
        w_hi_ready = sem("w_hi_ready")
        w_lo_ready = sem("w_lo_ready")
        setup_pool = sem("setup_pool")
        setup_ones = sem("setup_ones")
        setup_act = sem("setup_act")
        setup_dve = sem("setup_dve")
        b_low_moved = sem("b_low_moved")
        var_ready = sem("var_ready")
        rstd_ready = sem("rstd_ready")
        x_normed = sem("x_normed")
        q_hi_ready = sem("q_hi_ready")
        q_lo_ready = sem("q_lo_ready")
        q_turned = sem("q_turned")
        q_stacked = sem("q_stacked")
        v_ready = sem("v_ready")
        k_pos = sem("k_pos")
        k_hi_ready = sem("k_hi_ready")
        k_lo_ready = sem("k_lo_ready")
        s_ready = sem("s_ready")
        s_maxed = sem("s_maxed")
        m_hi_ready = sem("m_hi_ready")
        m_split = sem("m_split")
        m_turned = sem("m_turned")
        m_copied = sem("m_copied")
        st_ready = sem("st_ready")
        exp_ready = sem("exp_ready")
        p_summed = sem("p_summed")
        pv_ready = sem("pv_ready")
        rden_ready = sem("rden_ready")
        o_ready = sem("o_ready")
        o_written = sem("o_written")
        o_moved = sem("o_moved")
        o_hi_ready = sem("o_hi_ready")
        o_lo_ready = sem("o_lo_ready")
        z_ready = sem("z_ready")
        z_relued = sem("z_relued")
        x1_ready = sem("x1_ready")
        stat2 = sem("stat2")
        mv2 = sem("mv2")
        stat1 = sem("stat1")
        mv1 = sem("mv1")
        var2_ready = sem("var2_ready")
        rstd2_ready = sem("rstd2_ready")
        xn_ready = sem("xn_ready")
        xn_turned = sem("xn_turned")
        xt_ready = sem("xt_ready")
        xd_ready = sem("xd_ready")
        xk_ready = sem("xk_ready")
        xk_hi_ready = sem("xk_hi_ready")
        xk_lo_ready = sem("xk_lo_ready")
        xr_ready = sem("xr_ready")
        xr_hi_ready = sem("xr_hi_ready")
        xr_lo_ready = sem("xr_lo_ready")
        kt_ready = sem("kt_ready")
        kt_relued = sem("kt_relued")
        ka_ready = sem("ka_ready")
        ka_hi_ready = sem("ka_hi_ready")
        ka_lo_ready = sem("ka_lo_ready")
        r_ready = sem("r_ready")
        th_ready = sem("th_ready")
        vv_ready = sem("vv_ready")
        y_ready = sem("y_ready")
        out_ready = sem("out_ready")

        def after(eng, s, value):
            if not isinstance(value, int) or value > 0:
                eng.wait_ge(s, value)

        def on(b):
            return not isinstance(b, int) or 0 <= b < NB

        def half_weight(w, n):
            return w[n // 2][:, 2 * (n % 2):2 * (n % 2) + 2, :].rearrange("p c n -> p (c n)")

        def by_tile(o, u):
            return o[:, :, P * u:P * u + P].rearrange("p k (g a) -> p k g a", g=2 * GR)

        def pipeline(eng, iteration):
            for i in range(-1, 4):
                iteration(i, i % 2)
            with eng.Fori(6, NB // 2 + 3) as pair:
                iteration(pair * 2 - 8, 0)
                iteration(pair * 2 - 7, 1)
            for i in range(NB - 2, NB + 3):
                iteration(i, i % 2)

        block = es.enter_context(nc.Block())

        @block.sync
        def _(sp):
            def load_w(i):
                if isinstance(i, int) and i == -1:
                    sp.wait_ge(setup_dve, 1)
                    sp.dma_start(b_rows[1:2, :].bitcast(F32), b_low.bitcast(F32)).then_inc(b_low_moved, 16)
                    sp.wait_ge(b_low_moved, 16)
                    sp.wait_ge(setup_act, 3)
                    for n in range(8):
                        sp.dma_start(w_raw[n].rearrange("p (c n) -> p c n", c=2),
                                     w_t[n // 2].rearrange("(h c p) n -> h p c n", h=2, p=P)[n % 2]
                                     ).then_inc(w_loaded[n], 16)

            def load_x(b):
                if on(b):
                    after(sp, q_lo_ready, 2 * b)
                    after(sp, q_hi_ready, 2 * b)
                    for m in range(GR):
                        part = slice(P // 2 * (m % 2), P // 2 * (m % 2) + P // 2)
                        sp.dma_start(x_ln[part, m // 2, :],
                                     x[b].rearrange("(a k m) d -> m k a d", k=KC, m=GR)[m]).then_inc(x_loaded, 16)

            def load_k(b, c):
                if on(b):
                    after(sp, k_hi_ready, CH * b + c)
                    after(sp, k_lo_ready, CH * b + c)
                    for r in range(3):
                        sp.dma_start(k_raw[HD * r:HD * r + HD, :, :],
                                     ctx_t[b][:, GR * c:GR * c + GR, :]).then_inc(k_loaded, 16)

            def move_m(b, c):
                if on(b):
                    sp.wait_ge(m_copied, CH * b + c + 1)
                    for piece in range(2):
                        sp.dma_start(q_st[QK + piece:QK + piece + 1, c, :, :].bitcast(F32),
                                     m_t[GR * piece:GR * piece + GR, :].bitcast(F32)).then_inc(m_moved[c % 2], 16)

            def write_o(b, c):
                if on(b):
                    sp.wait_ge(o_ready, CH * b + c + 1)
                    sp.dma_start(o_dram[c].rearrange("g f m r -> (g f) (m r)"), o_val[:, :]).then_inc(o_written, 16)

            def read_o(b, u):
                if on(b):
                    sp.wait_ge(o_written, 16 * (CH * b + 2 * u + 2))
                    for m in range(GR):
                        sp.dma_start(o_mv[HD * m:HD * m + HD, :, :],
                                     o_dram[2 * u:2 * u + 2, :, :, m, :].rearrange("c g f r -> f (c g) r")
                                     ).then_inc(o_moved, 16)

            def store(b, par):
                if on(b):
                    sp.wait_ge(out_ready, NU * (b + 1))
                    sp.dma_start(out[b].rearrange("(u p) d -> p u d", p=P), x1[:, par, :, :]).then_inc(stored, 16)

            def iteration(i, par):
                load_k(i, 3)
                store(i - 3, 1 - par)
                move_m(i, 1)
                write_o(i - 1, 3)
                read_o(i - 1, 1)
                load_k(i + 1, 0)
                move_m(i, 2)
                write_o(i, 0)
                load_k(i + 1, 1)
                load_x(i + 2)
                move_m(i, 3)
                write_o(i, 1)
                load_k(i + 1, 2)
                move_m(i + 1, 0)
                load_w(i)
                read_o(i, 0)
                write_o(i, 2)

            load_x(0)
            sp.dma_start(mu_sb[:, 0, :], mu[0]).then_inc(setup_loaded, 16)
            sp.dma_start(mu_sb[:, 1, :], mu[1]).then_inc(setup_loaded, 16)
            for n, gate in enumerate((g_xattn, g_ffn)):
                sp.dma_start(gates[:, n:n + 1],
                             gate.rearrange("(a n) -> a n", a=1).broadcast_to([P, 1])).then_inc(setup_loaded, 16)
            sp.dma_start(b_raw, bias.rearrange("(a n) -> a n", a=1)).then_inc(setup_loaded, 16)
            pipeline(sp, iteration)
            sp.wait_ge(stored, 16 * NB)

        @block.gpsimd
        def _(pool):
            nc.gpsimd.memset(ident_raw, 0.0).then_inc(setup_pool, 1)
            pool.wait_ge(setup_pool, 1)
            nc.gpsimd.affine_select(out=ident_raw, in_=ident_raw, compare_op=ALU.not_equal, fill=1.0,
                                    base=0, pattern=[[-1, P]], channel_multiplier=1).then_inc(setup_pool, 1)
            pool.wait_ge(setup_ones, 1)

            def rstd_1(b):
                if on(b):
                    pool.wait_ge(var_ready, b + 1)
                    after(pool, x_normed, NU * b)
                    nc.gpsimd.tensor_tensor(rstd[:, 0, :], ve[:, 0, :], mhalf[:, 0:1].broadcast_to([P, NU]),
                                            ALU.pow).then_inc(rstd_ready, 1)

            def rstd_2(b, u):
                if on(b):
                    pool.wait_ge(var2_ready, NU * b + u + 1)
                    after(pool, xn_ready, NU * (b - 1) + u + 1)
                    nc.gpsimd.tensor_tensor(rstd[:, 1, u:u + 1], ve[:, 1, u:u + 1], mhalf[:, 0:1],
                                            ALU.pow).then_inc(rstd2_ready, 1)

            def k_low(b, c, *before):
                if on(b):
                    for batch, s, count in before:
                        if on(batch):
                            after(pool, s, count)
                    pool.wait_ge(k_pos, CH * b + c + 1)
                    pool.wait_ge(k_hi_ready, CH * b + c + 1)
                    rows = slice(2 * HD, 3 * HD)
                    nc.gpsimd.tensor_tensor(k_st[rows, c, :, :], k_raw[rows, :, :], k_st[rows, c, :, :].bitcast(F32),
                                            ALU.subtract).then_inc(k_lo_ready, 1)
                    pool.wait_ge(k_lo_ready, CH * b + c + 1)

            def p_add(b, c, half):
                if on(b):
                    pool.wait_ge(exp_ready, HEADS * b + GR * c + 2 * half + 2)
                    after(pool, pv_ready, CH * b + c)
                    two = slice(2 * half, 2 * half + 2)
                    nc.gpsimd.tensor_tensor(p_sum[:, two, :], probs[:, c % 2, two, 0, :], probs[:, c % 2, two, 1, :],
                                            ALU.add).then_inc(p_summed, 1)

            def o_low(b, u):
                if on(b):
                    pool.wait_ge(o_hi_ready, NU * b + u + 1)
                    after(pool, z_ready, NU * (b - 1) + u + 1)
                    nc.gpsimd.tensor_tensor(by_tile(o_lo, u), o_mv[:, :, :].rearrange("p g (k a) -> p k g a", k=KC),
                                            by_tile(o_hi, u).bitcast(F32), ALU.subtract).then_inc(o_lo_ready, 1)

            def x_diff(b, u):
                if on(b):
                    pool.wait_ge(xt_ready, NU * b + u + 1)
                    after(pool, xr_hi_ready, b)
                    after(pool, xr_lo_ready, b)
                    nc.gpsimd.tensor_tensor(xd[:, :, P * u:P * u + P], xt[:, :, 1 + P * u:1 + P * u + P],
                                            xt[:, :, P * u:P * u + P], ALU.subtract).then_inc(xd_ready, 1)

            def xk_low(b, half):
                if on(b):
                    pool.wait_ge(xk_ready, 2 * b + half + 1)
                    pool.wait_ge(xk_hi_ready, 2 * b + half + 1)
                    after(pool, kt_ready, 2 * b)
                    part = slice(2 * half, 2 * half + 2)
                    nc.gpsimd.tensor_tensor(xk_lo[:, part, :], xm[:, part, :], xk_hi[:, part, :].bitcast(F32),
                                            ALU.subtract).then_inc(xk_lo_ready, 1)

            def xr_low(b):
                if on(b):
                    pool.wait_ge(xr_ready, b + 1)
                    pool.wait_ge(xr_hi_ready, b + 1)
                    after(pool, r_ready, NU * b)
                    nc.gpsimd.tensor_tensor(xr_lo[:, :, :], xd[:, :, :], xr_hi[:, :, :].bitcast(F32),
                                            ALU.subtract).then_inc(xr_lo_ready, 1)

            def ka_square(b, half):
                if on(b):
                    pool.wait_ge(kt_relued, 2 * b + half + 1)
                    part = xm[:, 2 * half:2 * half + 2, :]
                    nc.gpsimd.tensor_tensor(part, part, part, ALU.mult).then_inc(ka_ready, 1)

            def ka_low(b, half):
                if on(b):
                    pool.wait_ge(ka_ready, 2 * b + half + 1)
                    pool.wait_ge(ka_hi_ready, 2 * b + half + 1)
                    after(pool, vv_ready, NU * b)
                    nc.gpsimd.tensor_tensor(ka_lo[:, 2 * half:2 * half + 2, :], xm[:, 2 * half:2 * half + 2, :],
                                            ka_hi[:, 2 * half:2 * half + 2, :].bitcast(F32),
                                            ALU.subtract).then_inc(ka_lo_ready, 1)

            def iteration(i, par):
                rstd_1(i + 1)
                k_low(i, 3,
                      (i + 1, rstd_ready, i + 2), (i - 1, o_lo_ready, 2 * (i - 1) + 1))
                ka_square(i - 2, 0)
                p_add(i, 0, 0)
                ka_square(i - 2, 1)
                p_add(i, 0, 1)
                o_low(i - 1, 1)
                xr_low(i - 2)
                k_low(i + 1, 0,
                      (i - 2, xr_lo_ready, i - 1), (i - 1, o_lo_ready, 2 * (i - 1) + 2),
                      (i, p_summed, 6 * i + 2), (i - 2, ka_ready, 2 * (i - 2) + 2))
                rstd_2(i - 1, 0)
                p_add(i, 1, 0)
                p_add(i, 1, 1)
                rstd_2(i - 1, 1)
                x_diff(i - 1, 0)
                ka_low(i - 2, 0)
                ka_low(i - 2, 1)
                x_diff(i - 1, 1)
                k_low(i + 1, 1,
                      (i - 1, xd_ready, 2 * (i - 1) + 2), (i - 2, ka_lo_ready, 2 * (i - 2) + 2),
                      (i - 1, rstd2_ready, 2 * (i - 1) + 2), (i, p_summed, 6 * i + 4))
                p_add(i, 2, 0)
                p_add(i, 2, 1)
                xk_low(i - 1, 0)
                xk_low(i - 1, 1)
                k_low(i + 1, 2,
                      (i - 1, xk_lo_ready, 2 * (i - 1) + 2), (i, p_summed, 6 * i + 6))
                o_low(i, 0)

            pipeline(pool, iteration)

        @block.scalar
        def _(act):
            act.wait_ge(setup_pool, 2)
            nc.scalar.activation(ident_r[:, :], ident_raw, ACT.Copy).then_inc(setup_act, 1)
            act.wait_ge(setup_ones, 1)
            act.wait_ge(setup_loaded, 80)
            nc.scalar.activation(tg[:, :], gates[:, :], ACT.Tanh).then_inc(setup_act, 1)
            nc.scalar.activation(b_rows[0:1, :], b_raw, ACT.Copy).then_inc(setup_act, 1)

            def split_high(i, n):
                if isinstance(i, int) and i == 0:
                    act.wait_ge(w_loaded[n], 16)
                    nc.scalar.activation(half_weight(w_hi, n), w_raw[n], ACT.Copy).then_inc(w_hi_ready, 1)

            def weights_split(i):
                if isinstance(i, int) and i == 1:
                    act.wait_ge(w_lo_ready, 8)

            def load_x1(b, par):
                if on(b):
                    after(act, stored, 16 * (b - 1))
                    act.dma_start(x1[:, par, :, :], x[b].rearrange("(u p) d -> p u d", p=P)).then_inc(x1_loaded, 16)

            def load_v(b):
                if on(b):
                    after(act, pv_ready, CH * b)
                    act.dma_start(v_pos[:, :, :], ctx_in[b].rearrange("(v p) d -> p v d", p=P)).then_inc(v_loaded, 16)

            def q_high(b, u):
                if on(b):
                    act.wait_ge(x_normed, NU * b + u + 1)
                    after(act, q_turned, 2 * CH * b)
                    xu = x_ln[:, u, :].rearrange("p (h f) -> p h f", h=HEADS)
                    nc.scalar.activation(q_nat[:, u, :, 0, :], xu, ACT.Relu)
                    nc.scalar.activation(q_nat[:, u, :, 2, :], xu, ACT.Relu).then_inc(q_hi_ready, 1)

            def q_stack(b, c, u):
                if on(b):
                    act.wait_ge(q_turned, 2 * CH * b + 2 * c + u + 1)
                    after(act, st_ready, HEADS * (b - 1) + GR * c + GR)
                    nc.scalar.activation(q_st[0:QK, c, :, P * u:P * u + P],
                                         tp_bank[0:QK, :].rearrange("p (g t) -> p g t", g=GR),
                                         ACT.Copy).then_inc(q_stacked, 1)

            def k_high(b, c):
                if on(b):
                    act.wait_ge(k_loaded, 48 * (CH * b + c + 1))
                    after(act, st_ready, HEADS * (b - 1) + GR * c + GR)
                    nc.scalar.activation(k_st[0:QK, c, :, :], k_raw[0:QK, :, :], ACT.Relu).then_inc(k_hi_ready, 1)
                    rows = slice(2 * HD, 3 * HD)
                    act.wait_ge(k_hi_ready, CH * b + c + 1)
                    nc.scalar.activation(k_raw[rows, :, :], k_raw[rows, :, :], ACT.Relu).then_inc(k_pos, 1)

            def exponent(b, n):
                if on(b):
                    act.wait_ge(st_ready, HEADS * b + n + 1)
                    if isinstance(b, int) and b == 0 and n == GR:
                        act.wait_ge(w_lo_ready, 2)
                    if n % GR == 0:
                        after(act, pv_ready, CH * b + n // GR - 1)
                    nc.scalar.activation(probs[:, n // GR % 2, n % GR, :, :].rearrange("p v t -> p (v t)"),
                                         st_bank[n % 2][:, :], ACT.Exp, scale=SCALE).then_inc(exp_ready, 1)

            def o_high(b, u):
                if on(b):
                    act.wait_ge(o_moved, 16 * GR * (NU * b + u + 1))
                    after(act, z_ready, NU * (b - 1) + u + 1)
                    nc.scalar.activation(by_tile(o_hi, u), o_mv[:, :, :].rearrange("p g (k a) -> p k g a", k=KC),
                                         ACT.Copy).then_inc(o_hi_ready, 1)

            def z_relu(b, u):
                if on(b):
                    act.wait_ge(z_ready, NU * b + u + 1)
                    after(act, xn_turned, NU * (b - 1) + u + 1)
                    nc.scalar.activation(xn[:, u, :], dense_bank[u][:, :], ACT.Relu).then_inc(z_relued, 1)

            def xt_copy(b, u):
                if on(b):
                    act.wait_ge(xn_turned, NU * b + u + 1)
                    after(act, xr_ready, b)
                    nc.scalar.activation(xt[:, :, 1 + P * u:1 + P * u + P],
                                         tp_bank[:, :].rearrange("p (c t) -> p c t", c=KC),
                                         ACT.Copy).then_inc(xt_ready, 1)

            def xk_high(b, half):
                if on(b):
                    act.wait_ge(xk_ready, 2 * b + half + 1)
                    after(act, kt_ready, 2 * b)
                    part = slice(2 * half, 2 * half + 2)
                    nc.scalar.activation(xk_hi[:, part, :], xm[:, part, :], ACT.Copy).then_inc(xk_hi_ready, 1)

            def xr_high(b):
                if on(b):
                    act.wait_ge(xr_ready, b + 1)
                    after(act, r_ready, NU * b)
                    nc.scalar.activation(xr_hi[:, :, :], xd[:, :, :], ACT.Copy).then_inc(xr_hi_ready, 1)

            def kt_relu(b, half):
                if on(b):
                    act.wait_ge(kt_ready, 2 * b + half + 1)
                    act.wait_ge(xk_lo_ready, 2 * b + 2)
                    nc.scalar.activation(xm[:, 2 * half:2 * half + 2, :].rearrange("p c t -> p (c t)"),
                                         dense_bank[half][:, :], ACT.Relu).then_inc(kt_relued, 1)

            def ka_high(b, half):
                if on(b):
                    act.wait_ge(ka_ready, 2 * b + half + 1)
                    after(act, vv_ready, NU * b)
                    nc.scalar.activation(ka_hi[:, 2 * half:2 * half + 2, :], xm[:, 2 * half:2 * half + 2, :],
                                         ACT.Copy).then_inc(ka_hi_ready, 1)

            def r_tanh(b, u):
                if on(b):
                    act.wait_ge(r_ready, NU * b + u + 1)
                    after(act, out_ready, NU * (b - 1) + u + 1)
                    nc.scalar.activation(th[:, u, :], dense_bank[u][:, :], ACT.Tanh,
                                         scale=0.5).then_inc(th_ready, 1)

            def iteration(i, par):
                weights_split(i)
                q_stack(i, 2, 1)
                exponent(i, 0)
                exponent(i, 1)
                split_high(i, 0)
                k_high(i, 3)
                q_stack(i, 3, 0)
                load_x1(i - 1, 1 - par)
                exponent(i, 2)
                split_high(i, 1)
                kt_relu(i - 2, 0)
                q_stack(i, 3, 1)
                split_high(i, 2)
                load_v(i)
                q_high(i + 1, 0)
                split_high(i, 3)
                exponent(i, 3)
                exponent(i, 4)
                kt_relu(i - 2, 1)
                q_high(i + 1, 1)
                o_high(i - 1, 1)
                exponent(i, 5)
                split_high(i, 4)
                xr_high(i - 2)
                exponent(i, 6)
                split_high(i, 5)
                z_relu(i - 1, 0)
                q_stack(i + 1, 0, 0)
                k_high(i + 1, 0)
                exponent(i, 7)
                split_high(i, 6)
                q_stack(i + 1, 0, 1)
                exponent(i, 8)
                split_high(i, 7)
                ka_high(i - 2, 0)
                z_relu(i - 1, 1)
                q_stack(i + 1, 1, 0)
                ka_high(i - 2, 1)
                exponent(i, 9)
                xt_copy(i - 1, 0)
                exponent(i, 10)
                r_tanh(i - 2, 0)
                xt_copy(i - 1, 1)
                k_high(i + 1, 1)
                exponent(i, 11)
                q_stack(i + 1, 1, 1)
                exponent(i, 12)
                xk_high(i - 1, 0)
                r_tanh(i - 2, 1)
                exponent(i, 13)
                xk_high(i - 1, 1)
                k_high(i + 1, 2)
                q_stack(i + 1, 2, 0)
                exponent(i, 14)
                exponent(i, 15)
                o_high(i, 0)

            pipeline(act, iteration)

        @block.vector
        def _(dve):
            nc.vector.memset(b_rows[:, :].bitcast(F32), 0.0)
            nc.vector.memset(ones_r[:, :].bitcast(F32), 1.0)
            nc.vector.memset(mhalf[:, :], -0.5)
            nc.vector.memset(xt[:, :, 0:1], 0.0)
            nc.vector.memset(k_st[QK:P, :, :, :].bitcast(F32), 1.0).then_inc(setup_ones, 1)

            def split_low(i, n):
                if isinstance(i, int) and i == 0:
                    dve.wait_ge(w_hi_ready, n + 1)
                    nc.vector.tensor_tensor(half_weight(w_lo, n), w_raw[n], half_weight(w_hi, n).bitcast(F32),
                                            ALU.subtract).then_inc(w_lo_ready, 1)

            def stats_1(b):
                if on(b):
                    dve.wait_ge(x_loaded, 16 * GR * (b + 1))
                    for u in range(NU):
                        last = nc.vector.bn_stats(st6[:, 0, u, :], x_ln[:, u, :])
                    last.then_inc(stat1, 1)
                    dve.wait_ge(stat1, b + 1)
                    nc.vector.memset(carrier[:, :], 0.0)
                    for u in range(NU):
                        last = nc.vector.bn_aggr(mv[:, 0, u, :], st6[:, 0, u, :])
                    last.then_inc(mv1, 1)
                    dve.wait_ge(mv1, b + 1)
                    after(dve, rstd_ready, b)
                    nc.vector.tensor_scalar(ve[:, 0, :], mv[:, 0, :, 1], LN_EPS, None, ALU.add).then_inc(var_ready, 1)

            def norm_1(b):
                if on(b):
                    dve.wait_ge(rstd_ready, b + 1)
                    for u in range(NU):
                        nc.vector.tensor_scalar(x_ln[:, u, :], x_ln[:, u, :], mv[:, 0, u, 0:1], rstd[:, 0, u:u + 1],
                                                ALU.subtract, ALU.mult).then_inc(x_normed, 1)

            def q_low(b, u):
                if on(b):
                    dve.wait_ge(q_hi_ready, NU * b + u + 1)
                    nc.vector.scalar_tensor_tensor(out=q_nat[:, u, :, 1, :],
                                                   in0=x_ln[:, u, :].rearrange("p (h f) -> p h f", h=HEADS), scalar=0.0,
                                                   in1=q_nat[:, u, :, 0, :].bitcast(F32), op0=ALU.max,
                                                   op1=ALU.subtract).then_inc(q_lo_ready, 1)

            def relu_v(b):
                if on(b):
                    dve.wait_ge(v_loaded, 16 * (b + 1))
                    nc.vector.tensor_scalar(v_pos[:, :, :], v_pos[:, :, :], 0.0, None, ALU.max).then_inc(v_ready, 1)

            def head_max(b, n):
                if on(b):
                    dve.wait_ge(s_ready, HEADS * b + n + 1)
                    if n % GR == 0:
                        after(dve, m_split, CH * b + n // GR)
                    nc.vector.tensor_reduce(nmax[:, :, n % GR:n % GR + 1],
                                            s_bank[n % 2][:, :].rearrange("p (u y) -> p u y", u=NU),
                                            AX_X, ALU.max, negate=True).then_inc(s_maxed, 1)

            def split_m(b, c):
                if on(b):
                    dve.wait_ge(s_maxed, HEADS * b + GR * c + GR)
                    after(dve, m_turned, CH * b + c)
                    nc.vector.tensor_copy(m_nat[:, :, 0, :], nmax[:, :, :]).then_inc(m_hi_ready, 1)
                    dve.wait_ge(m_hi_ready, CH * b + c + 1)
                    nc.vector.tensor_tensor(m_nat[:, :, 1, :], nmax[:, :, :], m_nat[:, :, 0, :].bitcast(F32),
                                            ALU.subtract).then_inc(m_split, 1)

            def copy_m(b, c):
                if on(b):
                    dve.wait_ge(m_turned, CH * b + c + 1)
                    after(dve, m_moved[(c + 1) % 2], 32 * (2 * b + (c + 1) // 2))
                    nc.vector.tensor_copy(m_t[0:2 * GR, :], tp_bank[0:2 * GR, 0:T]).then_inc(m_copied, 1)

            def norm_o(b, c):
                if on(b):
                    dve.wait_ge(pv_ready, CH * b + c + 1)
                    after(dve, o_written, 16 * (CH * b + c))
                    if c % 2 == 1:
                        after(dve, o_lo_ready, NU * b + c // 2)
                    nc.vector.reciprocal(o_val[:, :], pv_bank[:, T:2 * T]).then_inc(rden_ready, 1)
                    dve.wait_ge(rden_ready, CH * b + c + 1)
                    nc.vector.tensor_tensor(o_val[:, :], pv_bank[:, 0:T], o_val[:, :],
                                            ALU.mult).then_inc(o_ready, 1)

            def add_x(b, u, par):
                if on(b):
                    dve.wait_ge(z_relued, NU * b + u + 1)
                    dve.wait_ge(x1_loaded, 16 * (b + 1))
                    nc.vector.scalar_tensor_tensor(out=x1[:, par, u, :], in0=xn[:, u, :], scalar=tg[:, 0:1],
                                                   in1=x1[:, par, u, :], op0=ALU.mult, op1=ALU.add).then_inc(x1_ready, 1)
                    dve.wait_ge(x1_ready, NU * b + u + 1)
                    nc.vector.bn_stats(st6[:, 1, u, :], x1[:, par, u, :]).then_inc(stat2, 1)
                    dve.wait_ge(stat2, NU * b + u + 1)
                    nc.vector.memset(carrier[:, :], 0.0)
                    nc.vector.bn_aggr(mv[:, 1, u, :], st6[:, 1, u, :]).then_inc(mv2, 1)
                    dve.wait_ge(mv2, NU * b + u + 1)
                    after(dve, rstd2_ready, NU * (b - 1) + u + 1)
                    nc.vector.tensor_scalar(ve[:, 1, u:u + 1], mv[:, 1, u, 1:2], LN_EPS, None,
                                            ALU.add).then_inc(var2_ready, 1)

            def norm_2(b, u, par):
                if on(b):
                    dve.wait_ge(rstd2_ready, NU * b + u + 1)
                    nc.vector.tensor_scalar(xn[:, u, :], x1[:, par, u, :], mv[:, 1, u, 0:1], rstd[:, 1, u:u + 1],
                                            ALU.subtract, ALU.mult).then_inc(xn_ready, 1)

            def mix_k(b):
                if on(b):
                    dve.wait_ge(xd_ready, NU * (b + 1))
                    after(dve, ka_lo_ready, 2 * b)
                    for half in range(2):
                        for c in (2 * half, 2 * half + 1):
                            last = nc.vector.scalar_tensor_tensor(out=xm[:, c, :], in0=xd[:, c, :],
                                                                  scalar=mu_sb[:, 1, c:c + 1], in1=xt[:, c, 0:T],
                                                                  op0=ALU.mult, op1=ALU.add)
                        last.then_inc(xk_ready, 1)

            def mix_r(b):
                if on(b):
                    dve.wait_ge(xk_ready, 2 * (b + 1))
                    for c in range(KC):
                        last = nc.vector.scalar_tensor_tensor(out=xd[:, c, :], in0=xd[:, c, :], scalar=mu_sb[:, 0, c:c + 1],
                                                              in1=xt[:, c, 0:T], op0=ALU.mult, op1=ALU.add)
                    last.then_inc(xr_ready, 1)

            def finish(b, u, par):
                if on(b):
                    dve.wait_ge(vv_ready, NU * b + u + 1)
                    dve.wait_ge(th_ready, NU * b + u + 1)
                    nc.vector.scalar_tensor_tensor(out=th[:, u, :], in0=th[:, u, :], scalar=1.0,
                                                   in1=dense_bank[u][:, :], op0=ALU.add, op1=ALU.mult).then_inc(y_ready, 1)
                    dve.wait_ge(y_ready, NU * b + u + 1)
                    nc.vector.scalar_tensor_tensor(out=x1[:, par, u, :], in0=th[:, u, :], scalar=tgh[:, 0:1],
                                                   in1=x1[:, par, u, :], op0=ALU.mult, op1=ALU.add).then_inc(out_ready, 1)

            def iteration(i, par):
                head_max(i, 7)
                split_m(i, 1)
                finish(i - 3, 1, 1 - par)
                copy_m(i, 1)
                norm_o(i - 1, 3)
                mix_r(i - 2)
                split_low(i, 0)
                head_max(i, 8)
                norm_1(i + 1)
                split_low(i, 1)
                head_max(i, 9)
                head_max(i, 10)
                split_low(i, 2)
                q_low(i + 1, 0)
                head_max(i, 11)
                relu_v(i)
                split_m(i, 2)
                split_low(i, 3)
                head_max(i, 12)
                split_low(i, 4)
                copy_m(i, 2)
                q_low(i + 1, 1)
                norm_o(i, 0)
                head_max(i, 13)
                head_max(i, 14)
                add_x(i - 1, 0, 1 - par)
                split_low(i, 5)
                split_low(i, 6)
                head_max(i, 15)
                split_m(i, 3)
                norm_2(i - 1, 0, 1 - par)
                add_x(i - 1, 1, 1 - par)
                copy_m(i, 3)
                norm_2(i - 1, 1, 1 - par)
                head_max(i + 1, 0)
                split_low(i, 7)
                norm_o(i, 1)
                head_max(i + 1, 1)
                head_max(i + 1, 2)
                mix_k(i - 1)
                head_max(i + 1, 3)
                split_m(i + 1, 0)
                copy_m(i + 1, 0)
                head_max(i + 1, 4)
                stats_1(i + 2)
                finish(i - 2, 0, par)
                head_max(i + 1, 5)
                norm_o(i, 2)
                head_max(i + 1, 6)

            stats_1(0)
            dve.wait_ge(setup_act, 3)
            nc.vector.tensor_tensor(b_low, b_raw, b_rows[0:1, :].bitcast(F32), ALU.subtract).then_inc(setup_dve, 1)
            nc.vector.tensor_scalar(tgh[:, :], tg[:, 1:2], 0.5, None, ALU.mult).then_inc(setup_dve, 1)
            dve.wait_ge(setup_dve, 2)
            pipeline(dve, iteration)

        @block.tensor
        def _(pe):
            pe.wait_ge(setup_act, 1)
            pe.wait_ge(setup_ones, 1)

            def weights_split(i):
                if isinstance(i, int) and i == 1:
                    pe.wait_ge(setup_act, 3)
                    pe.wait_ge(b_low_moved, 16)
                    pe.wait_ge(w_hi_ready, 8)
                    pe.wait_ge(w_lo_ready, 8)

            def freed(*copies):
                for s, b, per, k in copies:
                    if on(b):
                        after(pe, s, b * per + k)
                        break

            def turn_q(b, c, u, *users):
                if on(b):
                    pe.wait_ge(q_hi_ready, NU * b + u + 1)
                    pe.wait_ge(q_lo_ready, NU * b + u + 1)
                    freed(*users)
                    for g in range(GR):
                        mm = nc.tensor.transpose(tp_bank[0:QK, P * g:P * g + P].bitcast(F32R),
                                                 q_nat[:, u, GR * c + g, :, :], ident_r[:, :])
                    mm.then_inc(q_turned, 1)

            def turn_m(b, c, *users):
                if on(b):
                    pe.wait_ge(m_split, CH * b + c + 1)
                    freed(*users)
                    for u in range(NU):
                        mm = nc.tensor.transpose(tp_bank[0:2 * GR, P * u:P * u + P].bitcast(F32R),
                                                 m_nat[:, u, :, :], ident_r[:, :])
                    mm.then_inc(m_turned, 1)

            def turn_xn(b, u, *users):
                if on(b):
                    pe.wait_ge(xn_ready, NU * b + u + 1)
                    freed(*users)
                    for c in range(KC):
                        mm = nc.tensor.transpose(tp_bank[:, P * c:P * c + P], xn[:, u, P * c:P * c + P],
                                                 ident_r[:, :].bitcast(F32))
                    mm.then_inc(xn_turned, 1)

            def scores(b, n):
                if on(b):
                    c, g = n // GR, n % GR
                    if g == 0:
                        pe.wait_ge(q_stacked, 2 * CH * b + 2 * c + 2)
                        pe.wait_ge(k_hi_ready, CH * b + c + 1)
                        pe.wait_ge(k_lo_ready, CH * b + c + 1)
                    after(pe, s_maxed, HEADS * b + n - 1)
                    for u in range(NU):
                        mm = nc.tensor.matmul(s_bank[n % 2][:, T * u:T * u + T], q_st[0:QK, c, g, P * u:P * u + P],
                                              k_st[0:QK, c, g, :], start=True, stop=True)
                    mm.then_inc(s_ready, 1)

            def shifted_scores(b, n):
                if on(b):
                    c, g = n // GR, n % GR
                    if g == 0:
                        pe.wait_ge(m_moved[c % 2], 32 * (2 * b + c // 2 + 1))
                    after(pe, exp_ready, HEADS * b + n - 1)
                    for v in range(NU):
                        mm = nc.tensor.matmul(st_bank[n % 2][:, T * v:T * v + T], k_st[0:ST, c, g, P * v:P * v + P],
                                              q_st[0:ST, c, g, :], start=True, stop=True)
                    mm.then_inc(st_ready, 1)

            def values(b, c):
                if on(b):
                    pe.wait_ge(exp_ready, HEADS * b + GR * c + GR)
                    pe.wait_ge(v_ready, b + 1)
                    after(pe, o_ready, CH * b + c)
                    for v in range(NU):
                        for g in range(GR):
                            h = GR * c + g
                            nc.tensor.matmul(pv_bank[HD * g:HD * g + HD, 0:T], v_pos[:, v, HD * h:HD * h + HD],
                                             probs[:, c % 2, g, v, :], start=(v == 0), stop=(v == NU - 1))

            def denominators(b, c):
                if on(b):
                    after(pe, o_ready, CH * b + c)
                    if c < CH - 1:
                        pe.wait_ge(p_summed, 2 * (CH - 1) * b + 2 * c + 2)
                        sums = [[p_sum[:, g, :] for g in range(GR)]]
                    else:
                        sums = [[probs[:, c % 2, g, v, :] for g in range(GR)] for v in range(NU)]
                    for n, per_head in enumerate(sums):
                        for g, moving in enumerate(per_head):
                            mm = nc.tensor.matmul(pv_bank[HD * g:HD * g + HD, T:2 * T], ones_r[:, 0:HD].bitcast(F32),
                                                  moving, start=(n == 0), stop=(n == len(sums) - 1))
                    mm.then_inc(pv_ready, 1)

            def product(dst, lhs, rhs, first, last):
                for n, (a, c) in enumerate(((0, 0), (1, 0), (0, 1))):
                    mm = nc.tensor.matmul(dst, lhs[a], rhs[c], start=first and n == 0, stop=last and n == 2)
                return mm

            def project(b, u, part, *users):
                if on(b):
                    if part == 0:
                        freed(*users)
                        nc.tensor.matmul(dense_bank[u][:, :], ones_r[:, :], b_rows[:, :], start=True, stop=False)
                        pe.wait_ge(o_hi_ready, NU * b + u + 1)
                        pe.wait_ge(o_lo_ready, NU * b + u + 1)
                    rows = slice(P * u, P * u + P)
                    mm = product(dense_bank[u][:, :], (o_hi[:, part, rows], o_lo[:, part, rows]),
                                 (w_hi[W_X][:, part, :], w_lo[W_X][:, part, :]), False, part == KC - 1)
                    if part == KC - 1:
                        mm.then_inc(z_ready, 1)

            def receptance(b, u, part, *users):
                if on(b):
                    if part == 0:
                        freed(*users)
                        pe.wait_ge(xr_hi_ready, b + 1)
                        pe.wait_ge(xr_lo_ready, b + 1)
                    rows = slice(P * u, P * u + P)
                    mm = product(dense_bank[u][:, :], (xr_hi[:, part, rows], xr_lo[:, part, rows]),
                                 (w_hi[W_R][:, part, :], w_lo[W_R][:, part, :]), part == 0, part == KC - 1)
                    if part == KC - 1:
                        mm.then_inc(r_ready, 1)

            def key(b, half, part, *users):
                if on(b):
                    if part == 0:
                        freed(*users)
                    if half == 0 and part < 2:
                        pe.wait_ge(xk_hi_ready, 2 * b + part + 1)
                        pe.wait_ge(xk_lo_ready, 2 * b + part + 1)
                    m = part // 2
                    n = 2 * half + m
                    cols = slice(P * n, P * n + P)
                    for kc in (2 * (part % 2), 2 * (part % 2) + 1):
                        mm = product(dense_bank[half][:, T * m:T * m + T],
                                     (w_hi[W_K][:, kc, cols], w_lo[W_K][:, kc, cols]),
                                     (xk_hi[:, kc, :], xk_lo[:, kc, :]), kc == 0, kc == KC - 1)
                    if part == 3:
                        mm.then_inc(kt_ready, 1)

            def value(b, u, part, *users):
                if on(b):
                    if part == 0:
                        freed(*users)
                    if part % 2 == 0:
                        pe.wait_ge(ka_hi_ready, 2 * b + part // 2 + 1)
                        pe.wait_ge(ka_lo_ready, 2 * b + part // 2 + 1)
                    rows = slice(P * u, P * u + P)
                    mm = product(dense_bank[u][:, :], (ka_hi[:, part, rows], ka_lo[:, part, rows]),
                                 (w_hi[W_V][:, part, :], w_lo[W_V][:, part, :]), part == 0, part == KC - 1)
                    if part == KC - 1:
                        mm.then_inc(vv_ready, 1)

            def iteration(i, par):
                def dense(q, part):
                    b1, b2, u = i - 1, i - 2, q % 2
                    if q < 2:
                        key(b2, u, part, (y_ready, i - 3, NU, u + 1), (z_relued, b2, NU, u + 1))
                    elif q < 4:
                        project(b1, u, part, (kt_relued, b2, 2, u + 1))
                    elif q < 6:
                        receptance(b2, u, part, (z_relued, b1, NU, u + 1), (kt_relued, b2, 2, u + 1))
                    else:
                        value(b2, u, part, (th_ready, b2, NU, u + 1))

                turns = [("q", i, 2, 1), ("m", i, 1, 0), ("q", i, 3, 0), ("q", i, 3, 1),
                         ("m", i, 2, 0), ("q", i + 1, 0, 0), ("q", i + 1, 0, 1), ("q", i + 1, 1, 0),
                         ("x", i - 1, 0, 0), ("m", i, 3, 0), ("x", i - 1, 0, 1), ("q", i + 1, 1, 1),
                         ("m", i + 1, 0, 0), ("q", i + 1, 2, 0)]

                def copy_of(kind, b, c, u):
                    if kind == "q":
                        return q_stacked, b, 2 * CH, 2 * c + u + 1
                    if kind == "m":
                        return m_copied, b, CH, c + 1
                    return xt_ready, b, NU, u + 1

                def turn(n):
                    kind, b, c, u = turns[n]
                    users = [copy_of(*t) for t in reversed(turns[:n])]
                    users += [copy_of(t[0], t[1] - 1, *t[2:]) for t in reversed(turns)]
                    if kind == "q":
                        turn_q(b, c, u, *users)
                    elif kind == "m":
                        turn_m(b, c, *users)
                    else:
                        turn_xn(b, u, *users)

                turn(0)
                shifted_scores(i, 0)
                weights_split(i)
                dense(0, 0)
                scores(i, 7)
                dense(0, 1)
                shifted_scores(i, 1)
                values(i - 1, 3)
                turn(1)
                denominators(i - 1, 3)
                dense(0, 2)
                scores(i, 8)
                dense(0, 3)
                turn(2)
                shifted_scores(i, 2)
                scores(i, 9)
                dense(1, 0)
                dense(1, 1)
                shifted_scores(i, 3)
                turn(3)
                dense(1, 2)
                scores(i, 10)
                dense(1, 3)
                shifted_scores(i, 4)
                dense(2, 0)
                scores(i, 11)
                dense(2, 1)
                shifted_scores(i, 5)
                dense(2, 2)
                scores(i, 12)
                dense(2, 3)
                values(i, 0)
                turn(4)
                denominators(i, 0)
                shifted_scores(i, 6)
                turn(5)
                dense(3, 0)
                scores(i, 13)
                shifted_scores(i, 7)
                dense(3, 1)
                dense(3, 2)
                scores(i, 14)
                turn(6)
                dense(3, 3)
                shifted_scores(i, 8)
                dense(4, 0)
                scores(i, 15)
                turn(7)
                dense(4, 1)
                shifted_scores(i, 9)
                dense(4, 2)
                values(i, 1)
                turn(8)
                scores(i + 1, 0)
                dense(4, 3)
                turn(9)
                shifted_scores(i, 10)
                dense(5, 0)
                denominators(i, 1)
                turn(10)
                scores(i + 1, 1)
                dense(5, 1)
                shifted_scores(i, 11)
                dense(5, 2)
                scores(i + 1, 2)
                dense(5, 3)
                turn(11)
                shifted_scores(i, 12)
                dense(6, 0)
                scores(i + 1, 3)
                dense(6, 1)
                shifted_scores(i, 13)
                dense(6, 2)
                values(i, 2)
                turn(12)
                scores(i + 1, 4)
                dense(6, 3)
                shifted_scores(i, 14)
                dense(7, 0)
                scores(i + 1, 5)
                denominators(i, 2)
                turn(13)
                dense(7, 1)
                shifted_scores(i, 15)
                dense(7, 2)
                scores(i + 1, 6)
                dense(7, 3)

            pipeline(pe, iteration)


def kernel(**inputs):
    import numpy as np
    import concourse.bacc as bacc
    from concourse.bass_utils import run_bass_kernel_spmd

    x = np.asarray(inputs["x"])
    ctx_in = np.asarray(inputs["ctx_1024"])
    nb, t, d = ctx_in.shape
    ctx_t = ctx_in.reshape(nb, t, HEADS, d // HEADS).transpose(0, 3, 2, 1)
    arrays = {
        "x": x,
        "ctx": ctx_in,
        "ctx_t": ctx_t,
        "g_xattn": np.asarray(inputs["g_xattn"]),
        "g_ffn": np.asarray(inputs["g_ffn"]),
        "w_x": np.asarray(inputs["L0_xattn_ffn_w"]).T,
        "w_r": np.asarray(inputs["L0_ffn_W_r"]).T,
        "w_k": np.asarray(inputs["L0_ffn_W_k"]).T,
        "w_v": np.asarray(inputs["L0_ffn_W_v"]).T,
        "bias": np.asarray(inputs["L0_xattn_ffn_b"]),
        "mu_r": np.asarray(inputs["L0_ffn_mu_r"]).reshape(-1, P).T,
        "mu_k": np.asarray(inputs["L0_ffn_mu_k"]).reshape(-1, P).T,
    }
    arrays = {name: np.ascontiguousarray(a) for name, a in arrays.items()}
    nc = bacc.Bacc("TRN2", target_bir_lowering=False, num_devices=1)
    h = {name: nc.dram_tensor(name + "_dram", a.shape, mybir.dt.from_np(a.dtype), kind="ExternalInput").ap()
         for name, a in arrays.items()}
    out = nc.dram_tensor("out_dram", x.shape, mybir.dt.from_np(x.dtype), kind="ExternalOutput").ap()
    flamingo_block(nc, h["x"], h["ctx"], h["ctx_t"], h["g_xattn"], h["g_ffn"],
                   [h["w_x"], h["w_r"], h["w_k"], h["w_v"]], h["bias"], [h["mu_r"], h["mu_k"]], out)
    r = run_bass_kernel_spmd(nc, [{name + "_dram": a for name, a in arrays.items()}], core_ids=[0])
    return r.results[0]["out_dram"]
```
